# Optimizing a Trainium2 kernel written in Bass

```python
import numpy as np
import jax
import jax.numpy as jnp

def _softmax(x, axis=-1):
    return jax.nn.softmax(x, axis=axis)

def _gelu(x):
    return jax.nn.gelu(x, approximate=True)

def _silu(x):
    return jax.nn.silu(x)

def _sigmoid(x):
    return jax.nn.sigmoid(x)

def _layernorm(x, axis=-1, eps=1e-05):
    m = jnp.mean(x, axis=axis, keepdims=True)
    v = jnp.var(x, axis=axis, keepdims=True)
    return (x - m) / jnp.sqrt(v + eps)

def _scatter_add(tgt, idx, src, axis=0):
    return tgt.at[idx].add(src)

def _segment_sum(src, seg, n):
    return jax.ops.segment_sum(src, seg, n)
kernel_name = 'mk_dlrm_tower_d1_rec_r8_1ddd2b'

def setup_inputs(seed: int=0):
    np.random.seed(seed)
    _w = jnp.asarray

    def _rec_inputs():
        import jax
        import jax.numpy as jnp
        _tk = jax.random.key(seed)
        dense_ctx = jax.random.normal(jax.random.fold_in(_tk, 190), (512, 16), jnp.float32)
        ids = jnp.stack([jax.random.randint(jax.random.fold_in(_tk, 200 + f), (512,), 0, v, jnp.int32) for f, v in enumerate([1000, 1250, 1250, 12500, 125000, 12500, 1250, 125000, 1250, 12500, 1000, 12500, 1250, 12500, 1250, 12500, 125000, 12500, 125000, 12500, 125000, 1000, 12500, 12500, 1250, 1000, 125000, 1250, 125000, 12500, 1000, 1250, 1000, 1250, 125000, 1000, 1000, 1250, 1250])], axis=1)
        tbl_0 = 0.05 * jax.random.normal(jax.random.fold_in(_tk, 500 + 0), (1000, 16), jnp.float32)
        tbl_1 = 0.05 * jax.random.normal(jax.random.fold_in(_tk, 500 + 1), (1250, 16), jnp.float32)
        tbl_2 = 0.05 * jax.random.normal(jax.random.fold_in(_tk, 500 + 2), (1250, 16), jnp.float32)
        tbl_3 = 0.05 * jax.random.normal(jax.random.fold_in(_tk, 500 + 3), (12500, 16), jnp.float32)
        tbl_4 = 0.05 * jax.random.normal(jax.random.fold_in(_tk, 500 + 4), (125000, 16), jnp.float32)
        tbl_5 = 0.05 * jax.random.normal(jax.random.fold_in(_tk, 500 + 5), (12500, 16), jnp.float32)
        tbl_6 = 0.05 * jax.random.normal(jax.random.fold_in(_tk, 500 + 6), (1250, 16), jnp.float32)
        tbl_7 = 0.05 * jax.random.normal(jax.random.fold_in(_tk, 500 + 7), (125000, 16), jnp.float32)
        tbl_8 = 0.05 * jax.random.normal(jax.random.fold_in(_tk, 500 + 8), (1250, 16), jnp.float32)
        tbl_9 = 0.05 * jax.random.normal(jax.random.fold_in(_tk, 500 + 9), (12500, 16), jnp.float32)
        tbl_10 = 0.05 * jax.random.normal(jax.random.fold_in(_tk, 500 + 10), (1000, 16), jnp.float32)
        tbl_11 = 0.05 * jax.random.normal(jax.random.fold_in(_tk, 500 + 11), (12500, 16), jnp.float32)
        tbl_12 = 0.05 * jax.random.normal(jax.random.fold_in(_tk, 500 + 12), (1250, 16), jnp.float32)
        tbl_13 = 0.05 * jax.random.normal(jax.random.fold_in(_tk, 500 + 13), (12500, 16), jnp.float32)
        tbl_14 = 0.05 * jax.random.normal(jax.random.fold_in(_tk, 500 + 14), (1250, 16), jnp.float32)
        tbl_15 = 0.05 * jax.random.normal(jax.random.fold_in(_tk, 500 + 15), (12500, 16), jnp.float32)
        tbl_16 = 0.05 * jax.random.normal(jax.random.fold_in(_tk, 500 + 16), (125000, 16), jnp.float32)
        tbl_17 = 0.05 * jax.random.normal(jax.random.fold_in(_tk, 500 + 17), (12500, 16), jnp.float32)
        tbl_18 = 0.05 * jax.random.normal(jax.random.fold_in(_tk, 500 + 18), (125000, 16), jnp.float32)
        tbl_19 = 0.05 * jax.random.normal(jax.random.fold_in(_tk, 500 + 19), (12500, 16), jnp.float32)
        tbl_20 = 0.05 * jax.random.normal(jax.random.fold_in(_tk, 500 + 20), (125000, 16), jnp.float32)
        tbl_21 = 0.05 * jax.random.normal(jax.random.fold_in(_tk, 500 + 21), (1000, 16), jnp.float32)
        tbl_22 = 0.05 * jax.random.normal(jax.random.fold_in(_tk, 500 + 22), (12500, 16), jnp.float32)
        tbl_23 = 0.05 * jax.random.normal(jax.random.fold_in(_tk, 500 + 23), (12500, 16), jnp.float32)
        tbl_24 = 0.05 * jax.random.normal(jax.random.fold_in(_tk, 500 + 24), (1250, 16), jnp.float32)
        tbl_25 = 0.05 * jax.random.normal(jax.random.fold_in(_tk, 500 + 25), (1000, 16), jnp.float32)
        tbl_26 = 0.05 * jax.random.normal(jax.random.fold_in(_tk, 500 + 26), (125000, 16), jnp.float32)
        tbl_27 = 0.05 * jax.random.normal(jax.random.fold_in(_tk, 500 + 27), (1250, 16), jnp.float32)
        tbl_28 = 0.05 * jax.random.normal(jax.random.fold_in(_tk, 500 + 28), (125000, 16), jnp.float32)
        tbl_29 = 0.05 * jax.random.normal(jax.random.fold_in(_tk, 500 + 29), (12500, 16), jnp.float32)
        tbl_30 = 0.05 * jax.random.normal(jax.random.fold_in(_tk, 500 + 30), (1000, 16), jnp.float32)
        tbl_31 = 0.05 * jax.random.normal(jax.random.fold_in(_tk, 500 + 31), (1250, 16), jnp.float32)
        tbl_32 = 0.05 * jax.random.normal(jax.random.fold_in(_tk, 500 + 32), (1000, 16), jnp.float32)
        tbl_33 = 0.05 * jax.random.normal(jax.random.fold_in(_tk, 500 + 33), (1250, 16), jnp.float32)
        tbl_34 = 0.05 * jax.random.normal(jax.random.fold_in(_tk, 500 + 34), (125000, 16), jnp.float32)
        tbl_35 = 0.05 * jax.random.normal(jax.random.fold_in(_tk, 500 + 35), (1000, 16), jnp.float32)
        tbl_36 = 0.05 * jax.random.normal(jax.random.fold_in(_tk, 500 + 36), (1000, 16), jnp.float32)
        tbl_37 = 0.05 * jax.random.normal(jax.random.fold_in(_tk, 500 + 37), (1250, 16), jnp.float32)
        tbl_38 = 0.05 * jax.random.normal(jax.random.fold_in(_tk, 500 + 38), (1250, 16), jnp.float32)
        _rk = jax.random.fold_in(_tk, 7)
        W_top1 = 0.05 * jax.random.normal(jax.random.fold_in(_tk, 801), (400, 512), jnp.float32)
        W_top2 = 0.0441942 * jax.random.normal(jax.random.fold_in(_tk, 802), (512, 256), jnp.float32)
        W_top3 = 0.0625 * jax.random.normal(jax.random.fold_in(_tk, 803), (256, 1), jnp.float32)
        b_top1 = jnp.zeros((512,), jnp.float32)
        b_top2 = jnp.zeros((256,), jnp.float32)
        return (dense_ctx, ids, tbl_0, tbl_1, tbl_2, tbl_3, tbl_4, tbl_5, tbl_6, tbl_7, tbl_8, tbl_9, tbl_10, tbl_11, tbl_12, tbl_13, tbl_14, tbl_15, tbl_16, tbl_17, tbl_18, tbl_19, tbl_20, tbl_21, tbl_22, tbl_23, tbl_24, tbl_25, tbl_26, tbl_27, tbl_28, tbl_29, tbl_30, tbl_31, tbl_32, tbl_33, tbl_34, tbl_35, tbl_36, tbl_37, tbl_38, W_top1, b_top1, W_top2, b_top2, W_top3)
    dense_ctx, ids, tbl_0, tbl_1, tbl_2, tbl_3, tbl_4, tbl_5, tbl_6, tbl_7, tbl_8, tbl_9, tbl_10, tbl_11, tbl_12, tbl_13, tbl_14, tbl_15, tbl_16, tbl_17, tbl_18, tbl_19, tbl_20, tbl_21, tbl_22, tbl_23, tbl_24, tbl_25, tbl_26, tbl_27, tbl_28, tbl_29, tbl_30, tbl_31, tbl_32, tbl_33, tbl_34, tbl_35, tbl_36, tbl_37, tbl_38, W_top1, b_top1, W_top2, b_top2, W_top3 = _rec_inputs()

    def _L0_rec_setup():
        import jax, jax.numpy as jnp
        import numpy as np
        B, F0, D = (256, 39, 16)
        CROSS = [128, 128, 128]
        key = jax.random.key(seed)
        k0, k1, k2, k3 = jax.random.split(key, 4)
        inputs = jax.random.normal(k0, (B, F0, D), dtype=jnp.float32)
        f0 = jax.random.normal(k1, (F0 * F0, CROSS[0]), dtype=jnp.float32) * 0.05
        f1 = jax.random.normal(k2, (CROSS[0] * F0, CROSS[1]), dtype=jnp.float32) * 0.05
        f2 = jax.random.normal(k3, (CROSS[1] * F0, CROSS[2]), dtype=jnp.float32) * 0.05
        return {'inputs': inputs, 'f0': f0, 'f1': f1, 'f2': f2}
    _L0_rec_all = _L0_rec_setup()
    _L0_rec_in = {k: v for k, v in _L0_rec_all.items() if k in ('f0', 'f1', 'f2')}
    del _L0_rec_all
    return {'dense_ctx': dense_ctx, 'ids': ids, 'tbl_0': tbl_0, 'tbl_1': tbl_1, 'tbl_2': tbl_2, 'tbl_3': tbl_3, 'tbl_4': tbl_4, 'tbl_5': tbl_5, 'tbl_6': tbl_6, 'tbl_7': tbl_7, 'tbl_8': tbl_8, 'tbl_9': tbl_9, 'tbl_10': tbl_10, 'tbl_11': tbl_11, 'tbl_12': tbl_12, 'tbl_13': tbl_13, 'tbl_14': tbl_14, 'tbl_15': tbl_15, 'tbl_16': tbl_16, 'tbl_17': tbl_17, 'tbl_18': tbl_18, 'tbl_19': tbl_19, 'tbl_20': tbl_20, 'tbl_21': tbl_21, 'tbl_22': tbl_22, 'tbl_23': tbl_23, 'tbl_24': tbl_24, 'tbl_25': tbl_25, 'tbl_26': tbl_26, 'tbl_27': tbl_27, 'tbl_28': tbl_28, 'tbl_29': tbl_29, 'tbl_30': tbl_30, 'tbl_31': tbl_31, 'tbl_32': tbl_32, 'tbl_33': tbl_33, 'tbl_34': tbl_34, 'tbl_35': tbl_35, 'tbl_36': tbl_36, 'tbl_37': tbl_37, 'tbl_38': tbl_38, 'W_top1': W_top1, 'b_top1': b_top1, 'W_top2': W_top2, 'b_top2': b_top2, 'W_top3': W_top3, 'L0_rec_f0': _L0_rec_in['f0'], 'L0_rec_f1': _L0_rec_in['f1'], 'L0_rec_f2': _L0_rec_in['f2']}

def reference(dense_ctx, ids, tbl_0, tbl_1, tbl_2, tbl_3, tbl_4, tbl_5, tbl_6, tbl_7, tbl_8, tbl_9, tbl_10, tbl_11, tbl_12, tbl_13, tbl_14, tbl_15, tbl_16, tbl_17, tbl_18, tbl_19, tbl_20, tbl_21, tbl_22, tbl_23, tbl_24, tbl_25, tbl_26, tbl_27, tbl_28, tbl_29, tbl_30, tbl_31, tbl_32, tbl_33, tbl_34, tbl_35, tbl_36, tbl_37, tbl_38, W_top1, b_top1, W_top2, b_top2, W_top3, L0_rec_f0, L0_rec_f1, L0_rec_f2):
    import jax
    import jax.numpy as jnp

    def _L0_rec_ref(inputs, f0, f1, f2):
        import jax, jax.numpy as jnp
        import numpy as np
        B, F0, D = (256, 39, 16)
        CROSS = [128, 128, 128]
        filters = [f0, f1, f2]
        x0 = inputs
        xk = inputs
        outs = []
        for W in filters:
            b, f, d = x0.shape
            g = xk.shape[1]
            z = jnp.einsum('bfd,bgd->bfgd', x0, xk).reshape(b, f * g, d)
            cur = jnp.einsum('bpd,pm->bmd', z, W)
            outs.append(cur)
            xk = cur
        result = jnp.concatenate(outs, axis=1)
        return jnp.sum(result, axis=-1)
    e = jnp.stack([tbl_0[ids[:, 0]], tbl_1[ids[:, 1]], tbl_2[ids[:, 2]], tbl_3[ids[:, 3]], tbl_4[ids[:, 4]], tbl_5[ids[:, 5]], tbl_6[ids[:, 6]], tbl_7[ids[:, 7]], tbl_8[ids[:, 8]], tbl_9[ids[:, 9]], tbl_10[ids[:, 10]], tbl_11[ids[:, 11]], tbl_12[ids[:, 12]], tbl_13[ids[:, 13]], tbl_14[ids[:, 14]], tbl_15[ids[:, 15]], tbl_16[ids[:, 16]], tbl_17[ids[:, 17]], tbl_18[ids[:, 18]], tbl_19[ids[:, 19]], tbl_20[ids[:, 20]], tbl_21[ids[:, 21]], tbl_22[ids[:, 22]], tbl_23[ids[:, 23]], tbl_24[ids[:, 24]], tbl_25[ids[:, 25]], tbl_26[ids[:, 26]], tbl_27[ids[:, 27]], tbl_28[ids[:, 28]], tbl_29[ids[:, 29]], tbl_30[ids[:, 30]], tbl_31[ids[:, 31]], tbl_32[ids[:, 32]], tbl_33[ids[:, 33]], tbl_34[ids[:, 34]], tbl_35[ids[:, 35]], tbl_36[ids[:, 36]], tbl_37[ids[:, 37]], tbl_38[ids[:, 38]]], axis=1)
    z = _L0_rec_ref(e, L0_rec_f0, L0_rec_f1, L0_rec_f2)
    z = z.reshape(z.shape[0], -1)
    h = jnp.concatenate([z, dense_ctx], axis=1)
    h = jnp.maximum(h @ W_top1 + b_top1, 0.0)
    h = jnp.maximum(h @ W_top2 + b_top2, 0.0)
    y = h @ W_top3
    return y

_drawn_inputs = setup_inputs


def setup_inputs(seed=0):
    import zlib

    import numpy as np

    out = dict(_drawn_inputs(seed))
    spreads = {'b_top1': (0.0, 0.6), 'b_top2': (0.0, 0.1)}
    factors = {'tbl_0': 4.593,
     'tbl_1': 5.155,
     'tbl_2': 5.023,
     'tbl_3': 4.905,
     'tbl_4': 4.878,
     'tbl_5': 5.109,
     'tbl_6': 4.906,
     'tbl_7': 4.78,
     'tbl_8': 4.949,
     'tbl_9': 4.424,
     'tbl_10': 4.877,
     'tbl_11': 4.765,
     'tbl_12': 4.492,
     'tbl_13': 4.493,
     'tbl_14': 4.725,
     'tbl_15': 4.924,
     'tbl_16': 5.169,
     'tbl_17': 4.747,
     'tbl_18': 4.815,
     'tbl_19': 5.303,
     'tbl_20': 5.017,
     'tbl_21': 4.696,
     'tbl_22': 4.456,
     'tbl_23': 4.802,
     'tbl_24': 4.504,
     'tbl_25': 4.468,
     'tbl_26': 5.062,
     'tbl_27': 4.918,
     'tbl_28': 4.463,
     'tbl_29': 4.828,
     'tbl_30': 5.002,
     'tbl_31': 4.539,
     'tbl_32': 4.792,
     'tbl_33': 4.65,
     'tbl_34': 4.544,
     'tbl_35': 4.587,
     'tbl_36': 4.71,
     'tbl_37': 4.894,
     'tbl_38': 5.054,
     'L0_rec_f1': 4.938,
     'L0_rec_f2': 8.0}
    for name, (base, spread) in spreads.items():
        noise = np.random.default_rng([zlib.crc32(name.encode()), seed]).standard_normal(out[name].shape)
        drawn = base * np.exp(spread * noise) if base else spread * noise
        out[name] = jnp.asarray(drawn.astype(out[name].dtype))
    for name, factor in factors.items():
        out[name] = (out[name] * factor).astype(out[name].dtype)
    return out
```

```python
import concourse.bass as bass
from concourse import mybir
from contextlib import ExitStack

F0, D, MAPS = 39, 16, 128
B, CB, SB = 512, 32, 8
CHUNKS = B // CB
COLS = CB * D
SUBS = CB // SB
BT, PER_BT = 128, 128 // CB
PARTS = 3
XR = PARTS * F0
SHIFTS = (F0 + 1) // 2
T0 = (SHIFTS + 2) // 3
T0_ROWS = [min(3, SHIFTS - 3 * t) * F0 for t in range(T0)]
FG = (F0 + 3) // 4
FG_ROWS = [32 * min(4, F0 - 4 * i) for i in range(FG)]
GG = MAPS // 32
HALVES = 2 * FG
RING = 4
H1, H2 = 512, 256

SEL_A = 0
SEL_B = SEL_A + 3 * F0
SEL_F = SEL_B + T0 * 3 * F0
SEL_3 = SEL_F + FG * 128
IDB = SEL_3 + F0 + 1
SEL_COLS = IDB + 128


def dlrm_tower(nc, dense_t, ids, tables, w0a, w0b, w1, w2, wt1, wt1d, wt2, wt3, bt1, bt2, sel, eye_mask, y):
    fp32, bf16, f32r, i32 = mybir.dt.float32, mybir.dt.bfloat16, mybir.dt.float32r, mybir.dt.int32
    ALU, ACT, AX = mybir.AluOpType, mybir.ActivationFunctionType, mybir.AxisListType

    with ExitStack() as ctx:
        def sb(name, shape, dt=fp32):
            return ctx.enter_context(nc.sbuf_tensor(name, shape, dt))

        def bank(name):
            return ctx.enter_context(nc.psum_tensor(name, [128, 512], fp32))

        def sem(name):
            return ctx.enter_context(nc.semaphore(name))

        sel_sb = sb("sel_sb", [128, SEL_COLS], bf16)
        sel_a = sel_sb[0:XR, SEL_A:SEL_A + 3 * F0]
        eye_sb = sb("eye_sb", [128, 128 + SB])
        eye = eye_sb[:, 0:128]
        mask = eye_sb[:, 128:128 + SB]
        w0_sb = sb("w0_sb", [3 * F0, T0, MAPS])
        w1_hi = sb("w1_hi", [128, FG * GG, MAPS], f32r)
        w1_lo = sb("w1_lo", [128, FG * GG, MAPS], f32r)
        w2_sb = sb("w2_sb", [128, F0, MAPS])
        wt1_sb = sb("wt1_sb", [128, 3, H1])
        wt1d_sb = sb("wt1d_sb", [D, H1])
        wt2_sb = sb("wt2_sb", [128, H1 // 128, H2])
        wt3_sb = sb("wt3_sb", [128, H2 // 128])
        bt1_sb = sb("bt1_sb", [128, H1 // 128])
        bt2_sb = sb("bt2_sb", [128, H2 // 128])
        dense_sb = sb("dense_sb", [D, B])
        ids_sb = sb("ids_sb", [128, B // BT, F0], i32)
        ids_now = sb("ids_now", [128, F0], i32)
        e_sb = sb("e_sb", [128, F0, D])
        e_rest = sb("e_rest", [128, D, F0])
        e_parts = sb("e_parts", [128, D, PARTS, F0], bf16)
        x0t = sb("x0t", [XR, 4, COLS], bf16)
        a_sb = sb("a_sb", [3 * F0, COLS])
        z0_sb = sb("z0_sb", [3 * F0, COLS])
        x1_sb = sb("x1_sb", [128, 2, COLS])
        x1_rep = sb("x1_rep", [128, 2, GG, COLS])
        z_sb = sb("z_sb", [128, RING, 2, COLS])
        z_hi = sb("z_hi", [128, RING, 2, COLS], f32r)
        z_lo = sb("z_lo", [128, RING, 2, COLS], f32r)
        x2_sb = sb("x2_sb", [128, COLS])
        x2t_sb = sb("x2t_sb", [128, 2, 128 + F0])
        diag_sb = sb("diag_sb", [128, 2, SB, F0])
        s_sb = sb("s_sb", [128, FG * GG, BT])
        out0 = sb("out0", [128, BT])
        out1 = sb("out1", [128, BT])
        out2 = sb("out2", [128, BT])
        h1_sb = sb("h1_sb", [128, H1 // 128, BT])
        h2_sb = sb("h2_sb", [128, H2 // 128, BT])
        y_sb = sb("y_sb", [1, B])
        w0_raw = z_sb[0:3 * F0, :, :, :].rearrange("p r j c -> p (r j c)")
        w0a_raw = w0_raw[:, 0:T0 * MAPS].rearrange("p (t m) -> p t m", t=T0)
        w0b_raw = w0_raw[:, T0 * MAPS:2 * T0 * MAPS].rearrange("p (t m) -> p t m", t=T0)

        rep_ps = [bank("rep_ps0"), bank("rep_ps1")]
        pair_ps = bank("pair_ps")
        x1_ps = bank("x1_ps")
        x2_ps = [bank("x2_ps0"), bank("x2_ps1")]
        turn_ps = bank("turn_ps")
        s_ps = bank("s_ps")

        consts_in = sem("consts_in")
        ids_in = sem("ids_in")
        w0_in = sem("w0_in")
        w1_in = sem("w1_in")
        late_in = sem("late_in")
        ids_moved = sem("ids_moved")
        e_in = sem("e_in")
        e_split = sem("e_split")
        e_step = sem("e_step")
        w0_ready = sem("w0_ready")
        w1_hi_ready = sem("w1_hi_ready")
        w1_lo_ready = sem("w1_lo_ready")
        turned = sem("turned")
        x0t_ready = sem("x0t_ready")
        a_done = sem("a_done")
        a_ready = sem("a_ready")
        pair_done = sem("pair_done")
        z0_ready = sem("z0_ready")
        x1_done = sem("x1_done")
        x1_ready = sem("x1_ready")
        x1_spread = [sem("x1_spread0"), sem("x1_spread1")]
        rep_done = sem("rep_done")
        z_ready = sem("z_ready")
        z_hi_ready = sem("z_hi_ready")
        z_lo_pool = sem("z_lo_pool")
        z_lo_dve = sem("z_lo_dve")
        l1_done = sem("l1_done")
        x2_ready = sem("x2_ready")
        sum0_done = sem("sum0_done")
        sum1_done = sem("sum1_done")
        x2t_done = sem("x2t_done")
        x2t_ready = sem("x2t_ready")
        diag_ready = sem("diag_ready")
        s_done = sem("s_done")
        s_ready = sem("s_ready")
        out2_done = sem("out2_done")
        out2_ready = sem("out2_ready")
        h1_done = sem("h1_done")
        h1_ready = sem("h1_ready")
        h2_done = sem("h2_done")
        h2_ready = sem("h2_ready")
        y_done = sem("y_done")
        y_ready = sem("y_ready")
        y_stored = sem("y_stored")

        LATE = 8
        SPREADS = 16 * GG * 4

        def exists(t, k):
            return not isinstance(t, int) or 0 <= 4 * t + k < CHUNKS

        def slots(eng, one):
            for k in (-2, -1, 0):
                one(0, k)
            with eng.Fori(0, B // BT - 1) as t:
                for k in range(1, PER_BT + 1):
                    one(t, k)
            for k in range(1, PER_BT + 1):
                one(B // BT - 1, k)

        block = ctx.enter_context(nc.Block())

        @block.sync
        def _(sp):
            sp.dma_start(sel_sb[:, :], sel.bitcast(bf16)).then_inc(consts_in, 16)
            sp.dma_start(eye_sb[:, :], eye_mask).then_inc(consts_in, 16)
            sp.dma_start(w0a_raw, w0a).then_inc(w0_in, 16)
            sp.dma_start(w0b_raw, w0b).then_inc(w0_in, 16)
            sp.dma_start(s_sb[:, :, :], w1).then_inc(w1_in, 16)
            sp.dma_start(w2_sb[:, :, :], w2).then_inc(late_in, 16)
            sp.dma_start(wt1_sb[:, :, :], wt1).then_inc(late_in, 16)
            sp.dma_start(wt1d_sb[:, :], wt1d).then_inc(late_in, 16)
            sp.dma_start(wt2_sb[:, :, :], wt2).then_inc(late_in, 16)
            sp.dma_start(wt3_sb[:, :], wt3).then_inc(late_in, 16)
            sp.dma_start(bt1_sb[:, :], bt1).then_inc(late_in, 16)
            sp.dma_start(bt2_sb[:, :], bt2).then_inc(late_in, 16)
            sp.dma_start(dense_sb[:, :], dense_t).then_inc(late_in, 16)

            def slot(t, k):
                n = k + 1
                if exists(t, n):
                    sp.wait_ge(x1_ready, 4 * t + n + 1)
                    for j in range(GG):
                        for r in range(4):
                            sp.dma_start(x1_rep[32 * r:32 * r + 32, n % 2, j, :],
                                         x1_sb[32 * j:32 * j + 32, n % 2, :]).then_inc(x1_spread[n % 2], 16)

            slots(sp, slot)
            sp.wait_ge(y_ready, B // BT)
            sp.dma_start(y, y_sb[:, :]).then_inc(y_stored, 16)
            sp.wait_ge(y_stored, 16)

        @block.gpsimd
        def _(pool):
            pool.dma_start(ids_sb[:, :, :], ids).then_inc(ids_in, 16)
            pool.wait_ge(ids_in, 16)

            def gather(t, part):
                if part == 0:
                    if not isinstance(t, int) or t > 0:
                        pool.wait_ge(e_in, 16 * F0 * t)
                        pool.wait_ge(e_split, t)
                    nc.gpsimd.tensor_copy(ids_now[:, :], ids_sb[:, bass.ds(t, 1), :].rearrange("p a f -> p (a f)"))\
                        .then_inc(ids_moved, 1)
                    return
                for f in range(3 * part - 3, min(3 * part, F0)):
                    pool.indirect_dma_start(
                        out=e_sb[:, f, :], out_offset=None, in_=tables[f],
                        in_offset=bass.IndirectOffsetOnAxis(ap=ids_now[:, f:f + 1], axis=0)).then_inc(e_in, 16)

            gather(0, 0)
            pool.wait_ge(ids_moved, 1)
            for part in range(1, HALVES):
                gather(0, part)

            def slot(t, k):
                for h in range(HALVES):
                    if k == 1 and h == 1 and exists(t, PER_BT):
                        pool.wait_ge(ids_moved, t + 2)
                    if exists(t, k + (h + 1) // HALVES):
                        n = HALVES * k + h + 1
                        pool.wait_ge(z_hi_ready, HALVES * 4 * t + n + 1)
                        if not isinstance(t, int) or HALVES * 4 * t + n >= RING:
                            pool.wait_ge(l1_done, HALVES * 4 * t + n + 1 - RING)
                        js = 2 - n % 2
                        nc.gpsimd.tensor_tensor(z_lo[:, n % RING, 0:js, :], z_sb[:, n % RING, 0:js, :],
                                                z_hi[:, n % RING, 0:js, :].bitcast(fp32),
                                                ALU.subtract).then_inc(z_lo_pool, 1)
                    if h % 3 == 1 and 4 <= h < 4 + 3 * SUBS and exists(t, k - 1):
                        s = (h - 4) // 3
                        pool.wait_ge(x2t_ready, SUBS * 4 * t + SUBS * (k - 1) + s + 1)
                        nc.gpsimd.tensor_tensor(
                            diag_sb[:, s % 2, :, :],
                            x2t_sb[:, s % 2, 128:128 + F0].rearrange("p (a f) -> p a f", a=1).broadcast_to([128, SB, F0]),
                            mask.rearrange("p (b a) -> p b a", a=1).broadcast_to([128, SB, F0]),
                            ALU.mult).then_inc(diag_ready, 1)
                    if k == 1 and exists(t, PER_BT):
                        gather(t + 1, h)

            slots(pool, slot)

        @block.scalar
        def _(act):
            act.wait_ge(w1_in, 16)
            nc.scalar.activation(w1_hi[:, :, :], s_sb[:, :, :], ACT.Copy).then_inc(w1_hi_ready, 1)

            def slot(t, k):
                for h in range(HALVES):
                    if exists(t, k + (h + 2) // HALVES):
                        n = HALVES * k + h + 2
                        act.wait_ge(z_ready, HALVES * 4 * t + n + 1)
                        if not isinstance(t, int) or HALVES * 4 * t + n >= RING:
                            act.wait_ge(l1_done, HALVES * 4 * t + n + 1 - RING)
                        nc.scalar.activation(z_hi[:, n % RING, :, :], z_sb[:, n % RING, :, :],
                                             ACT.Copy).then_inc(z_hi_ready, 1)
                    if h == 0 and exists(t, k - 1):
                        act.wait_ge(l1_done, HALVES * 4 * t + HALVES * k)
                        nc.scalar.activation(x2_sb[:, :], x2_ps[(k - 1) % 2][:, :], ACT.Copy).then_inc(x2_ready, 1)
                    if h % 3 == 0 and 3 <= h < 3 + 3 * SUBS and exists(t, k - 1):
                        s = (h - 3) // 3
                        act.wait_ge(x2t_done, SUBS * 4 * t + SUBS * (k - 1) + s + 1)
                        nc.scalar.activation(x2t_sb[:, s % 2, :], turn_ps[:, 0:128 + F0], ACT.Copy)\
                            .then_inc(x2t_ready, 1)
                    if h % 3 == 0 and 6 <= h < 6 + 3 * SUBS and exists(t, k - 1):
                        s = (h - 6) // 3
                        act.wait_ge(s_done, SUBS * 4 * t + SUBS * (k - 1) + s + 1)
                        at = (k - 1) % PER_BT * CB + s * SB
                        nc.scalar.activation(s_sb[:, 0:F0, at:at + SB].rearrange("p f b -> p b f"),
                                             s_ps[:, 0:SB * F0].rearrange("p (b f) -> p b f", b=SB),
                                             ACT.Copy).then_inc(s_ready, 1)
                    if h == 14 and exists(t, k + 1):
                        act.wait_ge(x1_done, 4 * t + k + 2)
                        if not isinstance(t, int) or 4 * t + k + 1 >= 2:
                            act.wait_ge(x1_spread[(k + 1) % 2], SPREADS * (2 * t) + SPREADS * ((k + 1) // 2))
                            act.wait_ge(sum0_done, 4 * t + k)
                        nc.scalar.activation(x1_sb[:, (k + 1) % 2, :], x1_ps[:, :], ACT.Copy).then_inc(x1_ready, 1)
                    if h == 16 and exists(t, k + 2):
                        act.wait_ge(turned, 4 * t + k + 3)
                        nc.scalar.activation(
                            x0t[:, (k + 2) % 4, :].rearrange("p (s d b) -> p d s b", s=SUBS, d=D),
                            turn_ps[0:XR, :].rearrange("p (d s b) -> p d s b", d=D, s=SUBS),
                            ACT.Copy).then_inc(x0t_ready, 1)
                    if h == 19 and exists(t, k + 2):
                        act.wait_ge(a_done, 4 * t + k + 3)
                        nc.scalar.activation(a_sb[:, :], pair_ps[0:3 * F0, :], ACT.Copy).then_inc(a_ready, 1)
                    if k == PER_BT and h == 17:
                        act.wait_ge(out2_done, t + 1)
                        nc.scalar.activation(out2[:, :], s_ps[:, 0:BT], ACT.Copy).then_inc(out2_ready, 1)
                if k == PER_BT:
                    act.wait_ge(late_in, 16 * LATE)
                    act.wait_ge(h1_done, t + 1)
                    for m in range(H1 // 128):
                        last = nc.scalar.activation(h1_sb[:, m, :], turn_ps[:, m * BT:(m + 1) * BT], ACT.Relu,
                                                    bias=bt1_sb[:, m:m + 1])
                    last.then_inc(h1_ready, 1)
                    act.wait_ge(h2_done, t + 1)
                    for m in range(H2 // 128):
                        last = nc.scalar.activation(h2_sb[:, m, :], s_ps[:, m * BT:(m + 1) * BT], ACT.Relu,
                                                    bias=bt2_sb[:, m:m + 1])
                    last.then_inc(h2_ready, 1)
                    act.wait_ge(y_done, t + 1)
                    row = t * BT if isinstance(t, int) else act.snap(t * BT)
                    nc.scalar.activation(y_sb[:, bass.ds(row, BT)], turn_ps[0:1, 0:BT], ACT.Copy).then_inc(y_ready, 1)

            slots(act, slot)

        @block.vector
        def _(dve):
            dve.wait_ge(w0_in, 32)
            nc.vector.tensor_tensor(w0_sb[:, :, :], w0a_raw, w0b_raw, ALU.add).then_inc(w0_ready, 1)
            dve.wait_ge(w1_hi_ready, 1)
            nc.vector.tensor_tensor(w1_lo[:, :, :], s_sb[:, :, :], w1_hi[:, :, :].bitcast(fp32),
                                    ALU.subtract).then_inc(w1_lo_ready, 1)
            e_df = e_sb[:, :, :].rearrange("p f d -> p d f")

            def split(t, step):
                if step == 0:
                    dve.wait_ge(e_in, 16 * F0 * t + 16 * F0)
                    if not isinstance(t, int) or t > 0:
                        dve.wait_ge(turned, 4 * t)
                    nc.vector.tensor_copy(e_parts[:, :, 0, :], e_df).then_inc(e_step, 1)
                    dve.wait_ge(e_step, 3 * t + 1)
                if step == 1:
                    nc.vector.tensor_tensor(e_rest[:, :, :], e_df, e_parts[:, :, 0, :], ALU.subtract).then_inc(e_step, 1)
                    dve.wait_ge(e_step, 3 * t + 2)
                if step == 2:
                    nc.vector.tensor_copy(e_parts[:, :, 1, :], e_rest[:, :, :]).then_inc(e_step, 1)
                    dve.wait_ge(e_step, 3 * t + 3)
                if step == 3:
                    nc.vector.tensor_tensor(e_parts[:, :, 2, :], e_rest[:, :, :], e_parts[:, :, 1, :],
                                            ALU.subtract).then_inc(e_split, 1)

            for step in range(4):
                split(0, step)

            def slot(t, k):
                for h in range(HALVES):
                    if exists(t, k + (h + 2) // HALVES):
                        n = HALVES * k + h + 2
                        i, jp = n % HALVES // 2, n % 2
                        dve.wait_ge(rep_done, FG * 4 * t + n // 2 + 1)
                        if h == HALVES - 2:
                            at = k + 1
                            dve.wait_ge(x1_spread[at % 2], SPREADS * (2 * t) + SPREADS * (at // 2 + 1))
                        if not isinstance(t, int) or HALVES * 4 * t + n >= RING:
                            dve.wait_ge(z_hi_ready, HALVES * 4 * t + n + 1 - RING)
                            dve.wait_ge(z_lo_pool, HALVES * 4 * t + n + 1 - RING)
                            if n % 2 == 1:
                                dve.wait_ge(z_lo_dve, FG * 4 * t + (n + 1 - RING) // 2)
                        nc.vector.tensor_tensor(
                            z_sb[:, n % RING, :, :],
                            rep_ps[n // 2 % 2][:, :].rearrange("p (a c) -> p a c", a=1).broadcast_to([128, 2, COLS]),
                            x1_rep[:, (k + (h + 2) // HALVES) % 2, 2 * jp:2 * jp + 2, :],
                            ALU.mult).then_inc(z_ready, 1)
                    if h % 2 == 0 and h < 2 * T0 and exists(t, k + 1):
                        i = h // 2
                        rows = T0_ROWS[i]
                        dve.wait_ge(pair_done, T0 * 4 * t + T0 * (k + 1) + i + 1)
                        nc.vector.tensor_tensor(z0_sb[0:rows, :], pair_ps[0:rows, :], a_sb[0:rows, :],
                                                ALU.mult).then_inc(z0_ready, 1)
                    if h % 2 == 1 and exists(t, k):
                        n = HALVES * k + h
                        dve.wait_ge(z_hi_ready, HALVES * 4 * t + n + 1)
                        if not isinstance(t, int) or HALVES * 4 * t + n >= RING:
                            dve.wait_ge(l1_done, HALVES * 4 * t + n + 1 - RING)
                        nc.vector.tensor_tensor(z_lo[:, n % RING, 1, :], z_sb[:, n % RING, 1, :],
                                                z_hi[:, n % RING, 1, :].bitcast(fp32),
                                                ALU.subtract).then_inc(z_lo_dve, 1)
                    if h == 3 and exists(t, k - 1):
                        at = (k - 1) % PER_BT * CB
                        dve.wait_ge(x1_ready, 4 * t + k)
                        nc.vector.tensor_reduce(
                            out0[:, at:at + CB].rearrange("p (s b) -> p s b", s=SUBS),
                            x1_sb[:, (k - 1) % 2, :].rearrange("p (s d b) -> p s b d", s=SUBS, d=D),
                            axis=AX.X, op=ALU.add).then_inc(sum0_done, 1)
                    if h == 7 and exists(t, k - 1):
                        at = (k - 1) % PER_BT * CB
                        dve.wait_ge(x2_ready, 4 * t + k)
                        nc.vector.tensor_reduce(
                            out1[:, at:at + CB].rearrange("p (s b) -> p s b", s=SUBS),
                            x2_sb[:, :].rearrange("p (s d b) -> p s b d", s=SUBS, d=D),
                            axis=AX.X, op=ALU.add).then_inc(sum1_done, 1)
                    if k == 2 and exists(t, PER_BT) and h in (5, 7, 9, 11):
                        split(t + 1, (h - 5) // 2)

            slots(dve, slot)

        @block.tensor
        def _(pe):
            pe.wait_ge(consts_in, 32)

            def slot(t, k):
                for h in range(HALVES):
                    i = h // 2
                    if h % 2 == 0 and exists(t, k + (i + 2) // FG):
                        g = FG * k + i + 2
                        at = (k + (i + 2) // FG) % 4
                        f = (i + 2) % FG
                        if g % FG == 0:
                            pe.wait_ge(x0t_ready, 4 * t + k + 2)
                        if not isinstance(t, int) or FG * 4 * t + g >= 2:
                            pe.wait_ge(z_ready, HALVES * 4 * t + 2 * (g - 1))
                        nc.tensor.matmul(rep_ps[g % 2][:, :], sel_sb[0:XR, SEL_F + 128 * f:SEL_F + 128 * (f + 1)],
                                         x0t[:, at, :], start=True, stop=True).then_inc(rep_done, 1)
                    if h % 2 == 0 and 1 <= i <= T0 and exists(t, k + 1):
                        rows = T0_ROWS[i - 1]
                        pe.wait_ge(z0_ready, T0 * 4 * t + T0 * (k + 1) + i)
                        if i == 1:
                            pe.wait_ge(w0_ready, 1)
                            if not isinstance(t, int) or 4 * t + k + 1 > 0:
                                pe.wait_ge(x1_ready, 4 * t + k + 1)
                        mm = nc.tensor.matmul(x1_ps[:, :], w0_sb[0:rows, i - 1, :], z0_sb[0:rows, :],
                                              start=(i == 1), stop=(i == T0))
                        if i == T0:
                            mm.then_inc(x1_done, 1)
                    if h % 2 == 0 and i < T0 and exists(t, k + 1):
                        rows = T0_ROWS[i]
                        if i == 0:
                            pe.wait_ge(a_ready, 4 * t + k + 2)
                        nc.tensor.matmul(pair_ps[0:rows, :],
                                         sel_sb[0:XR, SEL_B + 3 * F0 * i:SEL_B + 3 * F0 * i + rows],
                                         x0t[:, (k + 1) % 4, :], start=True, stop=True).then_inc(pair_done, 1)
                    if h % 3 == 2 and 2 <= h < 2 + 3 * SUBS and exists(t, k - 1):
                        s = (h - 2) // 3
                        if s == 0:
                            pe.wait_ge(x2_ready, 4 * t + k)
                            if exists(t, k + 1):
                                pe.wait_ge(x0t_ready, 4 * t + k + 2)
                        else:
                            pe.wait_ge(x2t_ready, SUBS * 4 * t + SUBS * (k - 1) + s)
                        nc.tensor.transpose(turn_ps[:, 0:128], x2_sb[:, 128 * s:128 * s + 128], eye)
                        nc.tensor.matmul(turn_ps[:, 128:128 + F0], x0t[:, (k - 1) % 4, 128 * s:128 * s + 128],
                                         sel_sb[0:XR, SEL_3:SEL_3 + F0], start=True, stop=True).then_inc(x2t_done, 1)
                    if h % 3 == 2 and 5 <= h < 5 + 3 * SUBS and exists(t, k - 1):
                        s = (h - 5) // 3
                        pe.wait_ge(diag_ready, SUBS * 4 * t + SUBS * (k - 1) + s + 1)
                        if s > 0:
                            pe.wait_ge(s_ready, SUBS * 4 * t + SUBS * (k - 1) + s)
                        nc.tensor.matmul(s_ps[:, 0:SB * F0], x2t_sb[:, s % 2, 0:128],
                                         diag_sb[:, s % 2, :, :].rearrange("p b f -> p (b f)"),
                                         start=True, stop=True).then_inc(s_done, 1)
                    if h == 15 and exists(t, k + 2):
                        q = (k + 2) % 4
                        if q == 0:
                            pe.wait_ge(e_split, t + (k + 2) // 4 + 1)
                        if exists(t, k - 1):
                            pe.wait_ge(x2t_ready, SUBS * 4 * t + SUBS * k)
                        for d in range(D):
                            mm = nc.tensor.matmul(turn_ps[0:XR, CB * d:CB * (d + 1)],
                                                  e_parts[CB * q:CB * (q + 1), d, :, :].rearrange("p a f -> p (a f)"),
                                                  sel_sb[CB * q:CB * (q + 1), IDB + CB * q:IDB + CB * (q + 1)],
                                                  start=True, stop=True)
                        mm.then_inc(turned, 1)
                    if h == 18 and exists(t, k + 2):
                        pe.wait_ge(x0t_ready, 4 * t + k + 3)
                        nc.tensor.matmul(pair_ps[0:3 * F0, :], sel_a, x0t[:, (k + 2) % 4, :],
                                         start=True, stop=True).then_inc(a_done, 1)
                    if k == PER_BT and h in (16, 17):
                        if h == 16:
                            pe.wait_ge(late_in, 16 * LATE)
                            pe.wait_ge(s_ready, SUBS * 4 * t + SUBS * PER_BT)
                        for f in (range(0, F0 // 2) if h == 16 else range(F0 // 2, F0)):
                            mm = nc.tensor.matmul(s_ps[:, 0:BT], w2_sb[:, f, :], s_sb[:, f, :],
                                                  start=(f == 0), stop=(f == F0 - 1))
                        if h == 17:
                            mm.then_inc(out2_done, 1)
                    if exists(t, k):
                        n = HALVES * k + h
                        if n == 0 and isinstance(t, int) and t == 0:
                            pe.wait_ge(w1_lo_ready, 1)
                        pe.wait_ge(z_lo_pool, HALVES * 4 * t + n + 1)
                        if h % 2 == 1:
                            pe.wait_ge(z_lo_dve, FG * 4 * t + (n + 1) // 2)
                        rows = FG_ROWS[i]
                        for jj in range(2):
                            w = GG * i + 2 * (h % 2) + jj
                            acc = x2_ps[k % 2][:, :]
                            hi, lo = z_hi[0:rows, n % RING, jj, :], z_lo[0:rows, n % RING, jj, :]
                            nc.tensor.matmul(acc, w1_hi[0:rows, w, :], hi, start=(w == 0), stop=False)
                            nc.tensor.matmul(acc, w1_hi[0:rows, w, :], lo, start=False, stop=False)
                            mm = nc.tensor.matmul(acc, w1_lo[0:rows, w, :], hi, start=False,
                                                  stop=(w == FG * GG - 1))
                        mm.then_inc(l1_done, 1)
                if k == PER_BT:
                    pe.wait_ge(out2_ready, t + 1)
                    pe.wait_ge(sum1_done, 4 * t + 4)
                    for m in range(H1 // 128):
                        cols = slice(m * 128, (m + 1) * 128)
                        to = turn_ps[:, m * BT:(m + 1) * BT]
                        nc.tensor.matmul(to, wt1_sb[:, 0, cols], out0[:, :], start=True, stop=False)
                        nc.tensor.matmul(to, wt1_sb[:, 1, cols], out1[:, :], start=False, stop=False)
                        nc.tensor.matmul(to, wt1_sb[:, 2, cols], out2[:, :], start=False, stop=False)
                        mm = nc.tensor.matmul(to, wt1d_sb[:, cols], dense_sb[:, bass.ds(t * BT, BT)],
                                              start=False, stop=True)
                    mm.then_inc(h1_done, 1)
                    pe.wait_ge(h1_ready, t + 1)
                    for m in range(H2 // 128):
                        for q in range(H1 // 128):
                            mm = nc.tensor.matmul(s_ps[:, m * BT:(m + 1) * BT], wt2_sb[:, q, m * 128:(m + 1) * 128],
                                                  h1_sb[:, q, :], start=(q == 0), stop=(q == H1 // 128 - 1))
                    mm.then_inc(h2_done, 1)
                    pe.wait_ge(h2_ready, t + 1)
                    for q in range(H2 // 128):
                        mm = nc.tensor.matmul(turn_ps[0:1, 0:BT], wt3_sb[:, q:q + 1], h2_sb[:, q, :],
                                              start=(q == 0), stop=(q == H2 // 128 - 1))
                    mm.then_inc(y_done, 1)

            slots(pe, slot)


def constants():
    import numpy as np
    one = 0x3F80
    sel = np.zeros((128, SEL_COLS), np.uint16)
    f = np.arange(F0)
    for part in range(PARTS):
        rows = part * F0 + f
        for s in range(3):
            sel[rows, SEL_A + s * F0 + f] = one
        for s in range(SHIFTS):
            sel[part * F0 + (f + s) % F0, SEL_B + s * F0 + f] = one
        for field in range(F0):
            sel[part * F0 + field, SEL_F + 32 * field:SEL_F + 32 * (field + 1)] = one
        sel[rows, SEL_3 + f] = one
    sel[np.arange(128), IDB + np.arange(128)] = one
    eye_mask = np.zeros((128, 128 + SB), np.float32)
    eye_mask[np.arange(128), np.arange(128)] = 1
    eye_mask[np.arange(128), 128 + np.arange(128) % SB] = 1
    return sel, eye_mask


def kernel(dense_ctx, ids, W_top1, b_top1, W_top2, b_top2, W_top3, L0_rec_f0, L0_rec_f1, L0_rec_f2, **tables):
    import numpy as np
    import concourse.bacc as bacc
    from concourse.bass_utils import run_bass_kernel_spmd

    sel, eye_mask = constants()
    f = np.arange(F0)

    def pair_rows(w, mirrored):
        out = np.zeros((3 * F0, T0, MAPS), np.float32)
        for s in range(1 if mirrored else 0, SHIFTS):
            g = (f + s) % F0
            out[s % 3 * F0 + f, s // 3] = w[g * F0 + f if mirrored else f * F0 + g]
        return out

    f0, f1, f2 = (np.asarray(a) for a in (L0_rec_f0, L0_rec_f1, L0_rec_f2))
    padded = np.zeros((4 * FG, MAPS, MAPS), np.float32)
    padded[0:F0] = f1.reshape(F0, MAPS, MAPS)
    arrays = {
        "dense_t": np.asarray(dense_ctx).T,
        "ids_in": np.asarray(ids).reshape(B // BT, BT, F0).transpose(1, 0, 2),
        "w0a": pair_rows(f0, False),
        "w0b": pair_rows(f0, True),
        "w1": padded.reshape(FG, 4, GG, 32, MAPS).transpose(1, 3, 0, 2, 4).reshape(128, FG * GG, MAPS),
        "w2": f2.reshape(F0, MAPS, MAPS).transpose(1, 0, 2),
        "wt1": np.asarray(W_top1)[0:3 * MAPS].reshape(3, MAPS, H1).transpose(1, 0, 2),
        "wt1d": np.asarray(W_top1)[3 * MAPS:],
        "wt2": np.asarray(W_top2).reshape(H1 // 128, 128, H2).transpose(1, 0, 2),
        "wt3": np.asarray(W_top3).reshape(H2 // 128, 128).T,
        "bt1": np.asarray(b_top1).reshape(H1 // 128, 128).T,
        "bt2": np.asarray(b_top2).reshape(H2 // 128, 128).T,
        "sel": sel,
        "eye_mask": eye_mask,
    }
    for i in range(F0):
        arrays[f"tbl_{i}"] = np.asarray(tables[f"tbl_{i}"])
    arrays = {"in_" + n: np.ascontiguousarray(a) for n, a in arrays.items()}

    nc = bacc.Bacc("TRN2", target_bir_lowering=False, num_devices=1)
    a = {n: nc.dram_tensor(n, x.shape, mybir.dt.from_np(x.dtype), kind="ExternalInput").ap() for n, x in arrays.items()}
    y = nc.dram_tensor("out_y", (1, B), mybir.dt.float32, kind="ExternalOutput").ap()
    dlrm_tower(nc, a["in_dense_t"], a["in_ids_in"], [a[f"in_tbl_{i}"] for i in range(F0)], a["in_w0a"], a["in_w0b"],
               a["in_w1"], a["in_w2"], a["in_wt1"], a["in_wt1d"], a["in_wt2"], a["in_wt3"], a["in_bt1"], a["in_bt2"],
               a["in_sel"], a["in_eye_mask"], y)
    r = run_bass_kernel_spmd(nc, [arrays], core_ids=[0])
    return r.results[0]["out_y"].reshape(B, 1)
```

```python
import concourse.bass as bass
from concourse import mybir
from contextlib import ExitStack

F0, D, MAPS = 39, 16, 128
B, CB, SB = 512, 32, 8
CHUNKS = B // CB
COLS = CB * D
SUBS = CB // SB
BT, PER_BT = 128, 128 // CB
PARTS = 3
XR = PARTS * F0
SHIFTS = (F0 + 1) // 2
T0 = (SHIFTS + 2) // 3
T0_ROWS = [min(3, SHIFTS - 3 * t) * F0 for t in range(T0)]
FG = (F0 + 3) // 4
FG_ROWS = [32 * min(4, F0 - 4 * i) for i in range(FG)]
GG = MAPS // 32
HALVES = 2 * FG
RING = 4
H1, H2 = 512, 256
POOL_LO = [(0, 1, 3, 4, 6, 7, 9, 11, 12, 14, 15, 16, 18, 19), (3, 5, 8, 11, 13, 15, 18),
           (1, 3, 6, 8, 10, 12, 14, 16, 18), (0, 2, 3, 5, 6, 8, 9, 11, 12, 14, 15, 17, 18)]
GATHER_PARTS = 32
AHEAD_Z, AHEAD_POOL, AHEAD_DVE = 3, 2, 1
PAIR_AT = (1, 2, 4, 5, 7, 8, 10)
X1_AT = (2, 4, 5, 7, 8, 10, 11)
TURN_AT, TURNED_AT, S_AT, S_COPY_AT = ([base + 2 * s for s in range(SUBS)] for base in (1, 2, 3, 4))
OUT2_AT, H1_AT, H2_AT, Y_AT = (11, 12, 13), 15, 17, 19


def x0_turn_at(k):
    return 17 if k % PER_BT == 2 else 12


def split_at(step):
    return 12 + step

SEL_A = 0
SEL_B = SEL_A + 3 * F0
SEL_F = SEL_B + T0 * 3 * F0
SEL_3 = SEL_F + FG * 128
IDB = SEL_3 + F0 + 1
SEL_COLS = IDB + 128


def dlrm_tower(nc, dense_t, ids, tables, w0a, w0b, w1, w2, wt1, wt1d, wt2, wt3, bt1, bt2, sel, eye_mask, y):
    fp32, bf16, f32r, i32 = mybir.dt.float32, mybir.dt.bfloat16, mybir.dt.float32r, mybir.dt.int32
    ALU, ACT, AX = mybir.AluOpType, mybir.ActivationFunctionType, mybir.AxisListType

    with ExitStack() as ctx:
        def sb(name, shape, dt=fp32):
            return ctx.enter_context(nc.sbuf_tensor(name, shape, dt))

        def bank(name):
            return ctx.enter_context(nc.psum_tensor(name, [128, 512], fp32))

        def sem(name):
            return ctx.enter_context(nc.semaphore(name))

        sel_sb = sb("sel_sb", [128, SEL_COLS], bf16)
        sel_a = sel_sb[0:XR, SEL_A:SEL_A + 3 * F0]
        eye_sb = sb("eye_sb", [128, 128 + SB])
        eye = eye_sb[:, 0:128]
        mask = eye_sb[:, 128:128 + SB]
        w0_sb = sb("w0_sb", [3 * F0, T0, MAPS])
        w1_hi = sb("w1_hi", [128, FG * GG, MAPS], f32r)
        w1_lo = sb("w1_lo", [128, FG * GG, MAPS], f32r)
        w2_sb = sb("w2_sb", [128, F0, MAPS])
        wt1_sb = sb("wt1_sb", [128, 3, H1])
        wt1d_sb = sb("wt1d_sb", [D, H1])
        wt2_sb = sb("wt2_sb", [128, H1 // 128, H2])
        wt3_sb = sb("wt3_sb", [128, H2 // 128])
        bt1_sb = sb("bt1_sb", [128, H1 // 128])
        bt2_sb = sb("bt2_sb", [128, H2 // 128])
        dense_sb = sb("dense_sb", [D, B])
        ids_sb = sb("ids_sb", [128, B // BT, F0], i32)
        ids_now = sb("ids_now", [128, F0], i32)
        e_sb = sb("e_sb", [128, F0, D])
        e_rest = sb("e_rest", [128, D, F0])
        e_parts = sb("e_parts", [128, D, PARTS, F0], bf16)
        x0t = sb("x0t", [XR, 4, COLS], bf16)
        a_sb = sb("a_sb", [3 * F0, COLS])
        z0_sb = sb("z0_sb", [3 * F0, COLS])
        x1_sb = sb("x1_sb", [128, 2, COLS])
        x1_rep = sb("x1_rep", [128, 2, GG, COLS])
        z_sb = sb("z_sb", [128, RING, 2, COLS])
        z_hi = sb("z_hi", [128, RING, 2, COLS], f32r)
        z_lo = sb("z_lo", [128, RING, 2, COLS], f32r)
        x2_sb = sb("x2_sb", [128, COLS])
        x2t_sb = sb("x2t_sb", [128, 2, 128 + F0 + 1])
        diag_sb = sb("diag_sb", [128, 2, SB, F0 + 1])
        s_sb = sb("s_sb", [128, FG * GG, BT])
        out0 = sb("out0", [128, BT])
        out2 = sb("out2", [128, BT])
        h1_sb = sb("h1_sb", [128, H1 // 128, BT])
        h2_sb = sb("h2_sb", [128, H2 // 128, BT])
        y_sb = sb("y_sb", [1, B])
        w0_raw = z_sb[0:3 * F0, :, :, :].rearrange("p r j c -> p (r j c)")
        w0a_raw = w0_raw[:, 0:T0 * MAPS].rearrange("p (t m) -> p t m", t=T0)
        w0b_raw = w0_raw[:, T0 * MAPS:2 * T0 * MAPS].rearrange("p (t m) -> p t m", t=T0)

        rep_ps = [bank("rep_ps0"), bank("rep_ps1")]
        pair_ps = bank("pair_ps")
        x1_ps = bank("x1_ps")
        x2_ps = [bank("x2_ps0"), bank("x2_ps1")]
        turn_ps = bank("turn_ps")
        s_ps = bank("s_ps")
        first_banks = [pair_ps, s_ps, x2_ps[0], x2_ps[1]]

        consts_in = sem("consts_in")
        ids_in = sem("ids_in")
        w0_in = sem("w0_in")
        w1_in = sem("w1_in")
        late_in = sem("late_in")
        ids_moved = sem("ids_moved")
        e_in = sem("e_in")
        e_split = sem("e_split")
        e_step = sem("e_step")
        w0_ready = sem("w0_ready")
        w1_hi_ready = sem("w1_hi_ready")
        w1_lo_ready = sem("w1_lo_ready")
        ones_ready = sem("ones_ready")
        turned = sem("turned")
        x0t_ready = sem("x0t_ready")
        a_done = sem("a_done")
        a_ready = sem("a_ready")
        pair_done = sem("pair_done")
        z0_ready = sem("z0_ready")
        x1_done = sem("x1_done")
        x1_ready = sem("x1_ready")
        x1_spread = [[sem(f"x1_spread{p}{jp}") for jp in range(2)] for p in range(2)]
        rep_done = sem("rep_done")
        z_ready = sem("z_ready")
        z_hi_ready = sem("z_hi_ready")
        z_lo_pool = sem("z_lo_pool")
        z_lo_dve = sem("z_lo_dve")
        l1_done = sem("l1_done")
        x2_ready = sem("x2_ready")
        sum0_done = sem("sum0_done")
        x2t_done = sem("x2t_done")
        x2t_ready = sem("x2t_ready")
        diag_ready = sem("diag_ready")
        s_done = sem("s_done")
        s_ready = sem("s_ready")
        out2_done = sem("out2_done")
        out2_ready = sem("out2_ready")
        h1_done = sem("h1_done")
        h1_ready = sem("h1_ready")
        h2_done = sem("h2_done")
        h2_ready = sem("h2_ready")
        y_done = sem("y_done")
        y_ready = sem("y_ready")
        y_stored = sem("y_stored")

        def on_pool(n):
            return n % HALVES in POOL_LO[n // HALVES % PER_BT]

        per_tile = {pool_has: sum(on_pool(n) == pool_has for n in range(HALVES * PER_BT)) for pool_has in (True, False)}

        def wait_z_lo(eng, t, n):
            mine = on_pool(n)
            whole = n // (HALVES * PER_BT)
            count = per_tile[mine] * whole + sum(on_pool(i) == mine for i in range(n - whole * HALVES * PER_BT + 1))
            eng.wait_ge(z_lo_pool if mine else z_lo_dve, per_tile[mine] * t + count)

        LATE = 8
        SPREADS = 16 * 2 * 4

        def exists(t, k):
            return not isinstance(t, int) or 0 <= 4 * t + k < CHUNKS

        def slots(eng, one, first=None):
            one(0, -2)
            if first:
                first()
            one(0, -1)
            one(0, 0)
            with eng.Fori(0, B // BT - 1) as t:
                for k in range(1, PER_BT + 1):
                    one(t, k)
            for k in range(1, PER_BT + 1):
                one(B // BT - 1, k)

        block = ctx.enter_context(nc.Block())

        @block.sync
        def _(sp):
            sp.dma_start(sel_sb[:, :], sel.bitcast(bf16)).then_inc(consts_in, 16)
            sp.dma_start(eye_sb[:, :], eye_mask).then_inc(consts_in, 16)
            sp.dma_start(w0a_raw, w0a).then_inc(w0_in, 16)
            sp.dma_start(w0b_raw, w0b).then_inc(w0_in, 16)
            sp.dma_start(s_sb[:, :, :], w1).then_inc(w1_in, 16)
            sp.dma_start(w2_sb[:, :, :], w2).then_inc(late_in, 16)
            sp.dma_start(wt1_sb[:, :, :], wt1).then_inc(late_in, 16)
            sp.dma_start(wt1d_sb[:, :], wt1d).then_inc(late_in, 16)
            sp.dma_start(wt2_sb[:, :, :], wt2).then_inc(late_in, 16)
            sp.dma_start(wt3_sb[:, :], wt3).then_inc(late_in, 16)
            sp.dma_start(bt1_sb[:, :], bt1).then_inc(late_in, 16)
            sp.dma_start(bt2_sb[:, :], bt2).then_inc(late_in, 16)
            sp.dma_start(dense_sb[:, :], dense_t).then_inc(late_in, 16)

            def slot(t, k):
                n = k + 1
                if exists(t, n):
                    sp.wait_ge(x1_ready, 4 * t + n + 1)
                    for j in range(GG):
                        for r in range(4):
                            sp.dma_start(x1_rep[32 * r:32 * r + 32, n % 2, j, :],
                                         x1_sb[32 * j:32 * j + 32, n % 2, :]).then_inc(x1_spread[n % 2][j // 2], 16)

            slots(sp, slot)
            sp.wait_ge(y_ready, B // BT)
            sp.dma_start(y, y_sb[:, :]).then_inc(y_stored, 16)
            sp.wait_ge(y_stored, 16)

        @block.gpsimd
        def _(pool):
            pool.dma_start(ids_sb[:, :, :], ids).then_inc(ids_in, 16)
            pool.wait_ge(ids_in, 16)

            def gather(t, part):
                if part == 0:
                    if not isinstance(t, int) or t > 0:
                        pool.wait_ge(e_in, 16 * F0 * t)
                        pool.wait_ge(e_split, t)
                    nc.gpsimd.tensor_copy(ids_now[:, :], ids_sb[:, bass.ds(t, 1), :].rearrange("p a f -> p (a f)"))\
                        .then_inc(ids_moved, 1)
                    return
                for f in range(F0 * (part - 1) // (GATHER_PARTS - 1), F0 * part // (GATHER_PARTS - 1)):
                    pool.indirect_dma_start(
                        out=e_sb[:, f, :], out_offset=None, in_=tables[f],
                        in_offset=bass.IndirectOffsetOnAxis(ap=ids_now[:, f:f + 1], axis=0)).then_inc(e_in, 16)

            gather(0, 0)
            for half in range(2):
                nc.gpsimd.memset(x2t_sb[:, half, 128 + F0:], 1.0).then_inc(ones_ready, 1)
            pool.wait_ge(ids_moved, 1)
            for part in range(1, GATHER_PARTS):
                gather(0, part)

            def slot(t, k):
                for h in range(HALVES):
                    if k == 1 and h == 1 and exists(t, PER_BT):
                        pool.wait_ge(ids_moved, t + 2)
                    if h in S_AT and exists(t, k - 1):
                        s = S_AT.index(h)
                        pool.wait_ge(x2t_ready, SUBS * 4 * t + SUBS * (k - 1) + s + 1)
                        nc.gpsimd.tensor_tensor(
                            diag_sb[:, s % 2, :, :],
                            x2t_sb[:, s % 2, 128:].rearrange("p (a f) -> p a f", a=1).broadcast_to([128, SB, F0 + 1]),
                            mask.rearrange("p (b a) -> p b a", a=1).broadcast_to([128, SB, F0 + 1]),
                            ALU.mult).then_inc(diag_ready, 1)
                    n = HALVES * k + h + AHEAD_POOL
                    if exists(t, k + (h + AHEAD_POOL) // HALVES) and on_pool(n):
                        pool.wait_ge(z_hi_ready, HALVES * 4 * t + n + 1)
                        if not isinstance(t, int) or HALVES * 4 * t + n >= RING:
                            pool.wait_ge(l1_done, HALVES * 4 * t + n + 1 - RING)
                        nc.gpsimd.tensor_tensor(z_lo[:, n % RING, :, :], z_sb[:, n % RING, :, :],
                                                z_hi[:, n % RING, :, :].bitcast(fp32),
                                                ALU.subtract).then_inc(z_lo_pool, 1)
                    if k == 1 and exists(t, PER_BT):
                        gather(t + 1, h)
                    if k == 2 and h < GATHER_PARTS - HALVES and exists(t, PER_BT):
                        gather(t + 1, HALVES + h)

            pool.wait_ge(ones_ready, 2)
            slots(pool, slot)

        @block.scalar
        def _(act):
            act.wait_ge(w1_in, 16)
            nc.scalar.activation(w1_hi[:, :, :], s_sb[:, :, :], ACT.Copy).then_inc(w1_hi_ready, 1)

            def slot(t, k):
                for h in range(HALVES):
                    if h == 0 and exists(t, k - 1):
                        act.wait_ge(l1_done, HALVES * 4 * t + HALVES * k)
                        nc.scalar.activation(x2_sb[:, :], x2_ps[(k - 1) % 2][:, :], ACT.Copy).then_inc(x2_ready, 1)
                    if h in TURNED_AT and exists(t, k - 1):
                        s = TURNED_AT.index(h)
                        act.wait_ge(x2t_done, SUBS * 4 * t + SUBS * (k - 1) + s + 1)
                        nc.scalar.activation(x2t_sb[:, s % 2, 0:128 + F0], turn_ps[:, 0:128 + F0], ACT.Copy)\
                            .then_inc(x2t_ready, 1)
                    if h in S_COPY_AT and exists(t, k - 1):
                        s = S_COPY_AT.index(h)
                        act.wait_ge(s_done, SUBS * 4 * t + SUBS * (k - 1) + s + 1)
                        at = (k - 1) % PER_BT * CB + s * SB
                        nc.scalar.activation(s_sb[:, 0:F0 + 1, at:at + SB].rearrange("p f b -> p b f"),
                                             s_ps[:, 0:SB * (F0 + 1)].rearrange("p (b f) -> p b f", b=SB),
                                             ACT.Copy).then_inc(s_ready, 1)
                    if h == X1_AT[-1] and exists(t, k + 1):
                        act.wait_ge(x1_done, 4 * t + k + 2)
                        if not isinstance(t, int) or 4 * t + k + 1 >= 2:
                            for jp in range(2):
                                act.wait_ge(x1_spread[(k + 1) % 2][jp], SPREADS * (2 * t) + SPREADS * ((k + 1) // 2))
                            act.wait_ge(sum0_done, 4 * t + k)
                        nc.scalar.activation(x1_sb[:, (k + 1) % 2, :], x1_ps[:, :], ACT.Copy).then_inc(x1_ready, 1)
                    if h == x0_turn_at(k) + 1 and exists(t, k + 2):
                        act.wait_ge(turned, 4 * t + k + 3)
                        nc.scalar.activation(
                            x0t[:, (k + 2) % 4, :].rearrange("p (s d b) -> p d s b", s=SUBS, d=D),
                            turn_ps[0:XR, :].rearrange("p (d s b) -> p d s b", d=D, s=SUBS),
                            ACT.Copy).then_inc(x0t_ready, 1)
                    if h == 19 and exists(t, k + 2):
                        act.wait_ge(a_done, 4 * t + k + 3)
                        nc.scalar.activation(a_sb[:, :], pair_ps[0:3 * F0, :], ACT.Copy).then_inc(a_ready, 1)
                    if k == PER_BT and h == OUT2_AT[-1] + 1:
                        act.wait_ge(out2_done, t + 1)
                        nc.scalar.activation(out2[:, :], s_ps[:, 0:BT], ACT.Copy).then_inc(out2_ready, 1)
                    if k == PER_BT and h == H1_AT + 1:
                        act.wait_ge(late_in, 16 * LATE)
                        act.wait_ge(h1_done, t + 1)
                        for m in range(H1 // 128):
                            last = nc.scalar.activation(h1_sb[:, m, :], turn_ps[:, m * BT:(m + 1) * BT], ACT.Relu,
                                                        bias=bt1_sb[:, m:m + 1])
                        last.then_inc(h1_ready, 1)
                    if k == PER_BT and h == H2_AT + 1:
                        act.wait_ge(h2_done, t + 1)
                        for m in range(H2 // 128):
                            last = nc.scalar.activation(h2_sb[:, m, :], s_ps[:, m * BT:(m + 1) * BT], ACT.Relu,
                                                        bias=bt2_sb[:, m:m + 1])
                        last.then_inc(h2_ready, 1)
                    n = HALVES * k + h + AHEAD_Z
                    if exists(t, k + (h + AHEAD_Z) // HALVES):
                        act.wait_ge(z_ready, HALVES * 4 * t + n + 1)
                        if not isinstance(t, int) or HALVES * 4 * t + n >= RING:
                            act.wait_ge(l1_done, HALVES * 4 * t + n + 1 - RING)
                        nc.scalar.activation(z_hi[:, n % RING, :, :], z_sb[:, n % RING, :, :],
                                             ACT.Copy).then_inc(z_hi_ready, 1)
                if k == PER_BT:
                    act.wait_ge(y_done, t + 1)
                    row = t * BT if isinstance(t, int) else act.snap(t * BT)
                    nc.scalar.activation(y_sb[:, bass.ds(row, BT)], turn_ps[0:1, 0:BT], ACT.Copy).then_inc(y_ready, 1)

            slots(act, slot)

        @block.vector
        def _(dve):
            dve.wait_ge(w0_in, 32)
            nc.vector.tensor_tensor(w0_sb[:, :, :], w0a_raw, w0b_raw, ALU.add).then_inc(w0_ready, 1)
            dve.wait_ge(w1_hi_ready, 1)
            nc.vector.tensor_tensor(w1_lo[:, :, :], s_sb[:, :, :], w1_hi[:, :, :].bitcast(fp32),
                                    ALU.subtract).then_inc(w1_lo_ready, 1)
            e_df = e_sb[:, :, :].rearrange("p f d -> p d f")

            def split(t, step):
                if step == 0:
                    dve.wait_ge(e_in, 16 * F0 * t + 16 * F0)
                    if not isinstance(t, int) or t > 0:
                        dve.wait_ge(turned, 4 * t)
                    nc.vector.tensor_copy(e_parts[:, :, 0, :], e_df).then_inc(e_step, 1)
                    dve.wait_ge(e_step, 3 * t + 1)
                if step == 1:
                    nc.vector.tensor_tensor(e_rest[:, :, :], e_df, e_parts[:, :, 0, :], ALU.subtract).then_inc(e_step, 1)
                    dve.wait_ge(e_step, 3 * t + 2)
                if step == 2:
                    nc.vector.tensor_copy(e_parts[:, :, 1, :], e_rest[:, :, :]).then_inc(e_step, 1)
                    dve.wait_ge(e_step, 3 * t + 3)
                if step == 3:
                    nc.vector.tensor_tensor(e_parts[:, :, 2, :], e_rest[:, :, :], e_parts[:, :, 1, :],
                                            ALU.subtract).then_inc(e_split, 1)

            for step in range(4):
                split(0, step)

            def slot(t, k):
                for h in range(HALVES):
                    if exists(t, k + (h + AHEAD_Z) // HALVES):
                        n = HALVES * k + h + AHEAD_Z
                        i, jp = n % HALVES // 2, n % 2
                        dve.wait_ge(rep_done, FG * 4 * t + n // 2 + 1)
                        if n % HALVES < 2:
                            at = k + 1
                            dve.wait_ge(x1_spread[at % 2][jp], SPREADS * (2 * t) + SPREADS * (at // 2 + 1))
                        if not isinstance(t, int) or HALVES * 4 * t + n >= RING:
                            dve.wait_ge(z_hi_ready, HALVES * 4 * t + n + 1 - RING)
                            wait_z_lo(dve, t, n - RING)
                        nc.vector.tensor_tensor(
                            z_sb[:, n % RING, :, :],
                            rep_ps[n // 2 % 2][:, :].rearrange("p (a c) -> p a c", a=1).broadcast_to([128, 2, COLS]),
                            x1_rep[:, n // HALVES % 2, 2 * jp:2 * jp + 2, :],
                            ALU.mult).then_inc(z_ready, 1)
                    if h in PAIR_AT and k != -1 and exists(t, k + 1):
                        i = PAIR_AT.index(h)
                        rows = T0_ROWS[i]
                        dve.wait_ge(pair_done, T0 * 4 * t + T0 * (k + 1) + i + 1)
                        nc.vector.tensor_tensor(z0_sb[0:rows, :], pair_ps[0:rows, :], a_sb[0:rows, :],
                                                ALU.mult).then_inc(z0_ready, 1)
                    n = HALVES * k + h + AHEAD_DVE
                    if exists(t, k + (h + AHEAD_DVE) // HALVES) and not on_pool(n):
                        dve.wait_ge(z_hi_ready, HALVES * 4 * t + n + 1)
                        if not isinstance(t, int) or HALVES * 4 * t + n >= RING:
                            dve.wait_ge(l1_done, HALVES * 4 * t + n + 1 - RING)
                        nc.vector.tensor_tensor(z_lo[:, n % RING, :, :], z_sb[:, n % RING, :, :],
                                                z_hi[:, n % RING, :, :].bitcast(fp32),
                                                ALU.subtract).then_inc(z_lo_dve, 1)
                    if h == 3 and exists(t, k - 1):
                        at = (k - 1) % PER_BT * CB
                        dve.wait_ge(x1_ready, 4 * t + k)
                        nc.vector.tensor_reduce(
                            out0[:, at:at + CB].rearrange("p (s b) -> p s b", s=SUBS),
                            x1_sb[:, (k - 1) % 2, :].rearrange("p (s d b) -> p s b d", s=SUBS, d=D),
                            axis=AX.X, op=ALU.add).then_inc(sum0_done, 1)
                    if k == 2 and exists(t, PER_BT) and split_at(0) <= h <= split_at(3):
                        split(t + 1, h - split_at(0))

            def first_pairs():
                dve.wait_ge(w0_ready, 1)
                dve.wait_ge(a_ready, 1)
                for i, rows in enumerate(T0_ROWS):
                    dve.wait_ge(pair_done, i + 1)
                    nc.vector.tensor_tensor(z_sb[0:rows, i // 2, i % 2, :], first_banks[i % 4][0:rows, :],
                                            a_sb[0:rows, :], ALU.mult).then_inc(z0_ready, 1)

            slots(dve, slot, first_pairs)

        @block.tensor
        def _(pe):
            pe.wait_ge(consts_in, 32)

            def slot(t, k):
                for h in range(HALVES):
                    i = h // 2
                    if h % 2 == 0 and exists(t, k + (i + 2) // FG):
                        g = FG * k + i + 2
                        at = (k + (i + 2) // FG) % 4
                        f = (i + 2) % FG
                        if g % FG == 0:
                            pe.wait_ge(x0t_ready, 4 * t + k + 2)
                        if not isinstance(t, int) or FG * 4 * t + g >= 2:
                            pe.wait_ge(z_ready, HALVES * 4 * t + 2 * (g - 1))
                        nc.tensor.matmul(rep_ps[g % 2][:, :], sel_sb[0:XR, SEL_F + 128 * f:SEL_F + 128 * (f + 1)],
                                         x0t[:, at, :], start=True, stop=True).then_inc(rep_done, 1)
                    if h in X1_AT and k != -1 and exists(t, k + 1):
                        q = X1_AT.index(h)
                        rows = T0_ROWS[q]
                        pe.wait_ge(z0_ready, T0 * 4 * t + T0 * (k + 1) + q + 1)
                        if q == 0:
                            pe.wait_ge(x1_ready, 4 * t + k + 1)
                        mm = nc.tensor.matmul(x1_ps[:, :], w0_sb[0:rows, q, :], z0_sb[0:rows, :],
                                              start=(q == 0), stop=(q == T0 - 1))
                        if q == T0 - 1:
                            mm.then_inc(x1_done, 1)
                    if h in PAIR_AT and k != -1 and exists(t, k + 1):
                        q = PAIR_AT.index(h)
                        rows = T0_ROWS[q]
                        if q == 0:
                            pe.wait_ge(a_ready, 4 * t + k + 2)
                        nc.tensor.matmul(pair_ps[0:rows, :],
                                         sel_sb[0:XR, SEL_B + 3 * F0 * q:SEL_B + 3 * F0 * q + rows],
                                         x0t[:, (k + 1) % 4, :], start=True, stop=True).then_inc(pair_done, 1)
                    if h in TURN_AT and exists(t, k - 1):
                        s = TURN_AT.index(h)
                        if s == 0:
                            pe.wait_ge(x2_ready, 4 * t + k)
                            if exists(t, k + 1):
                                pe.wait_ge(x0t_ready, 4 * t + k + 2)
                        else:
                            pe.wait_ge(x2t_ready, SUBS * 4 * t + SUBS * (k - 1) + s)
                        nc.tensor.transpose(turn_ps[:, 0:128], x2_sb[:, 128 * s:128 * s + 128], eye)
                        nc.tensor.matmul(turn_ps[:, 128:128 + F0], x0t[:, (k - 1) % 4, 128 * s:128 * s + 128],
                                         sel_sb[0:XR, SEL_3:SEL_3 + F0], start=True, stop=True).then_inc(x2t_done, 1)
                    if h == x0_turn_at(k) and exists(t, k + 2):
                        q = (k + 2) % 4
                        if q == 0:
                            pe.wait_ge(e_split, t + (k + 2) // 4 + 1)
                        if exists(t, k - 1):
                            pe.wait_ge(x2t_ready, SUBS * 4 * t + SUBS * k)
                        for d in range(D):
                            mm = nc.tensor.matmul(turn_ps[0:XR, CB * d:CB * (d + 1)],
                                                  e_parts[CB * q:CB * (q + 1), d, :, :].rearrange("p a f -> p (a f)"),
                                                  sel_sb[CB * q:CB * (q + 1), IDB + CB * q:IDB + CB * (q + 1)],
                                                  start=True, stop=True)
                        mm.then_inc(turned, 1)
                    if h == 19 and exists(t, k + 2):
                        pe.wait_ge(x0t_ready, 4 * t + k + 3)
                        nc.tensor.matmul(pair_ps[0:3 * F0, :], sel_a, x0t[:, (k + 2) % 4, :],
                                         start=True, stop=True).then_inc(a_done, 1)
                    if k == PER_BT and h in OUT2_AT:
                        q = OUT2_AT.index(h)
                        if q == 0:
                            pe.wait_ge(late_in, 16 * LATE)
                            pe.wait_ge(s_ready, SUBS * 4 * t + SUBS * PER_BT)
                        for f in range(F0 * q // len(OUT2_AT), F0 * (q + 1) // len(OUT2_AT)):
                            mm = nc.tensor.matmul(s_ps[:, 0:BT], w2_sb[:, f, :], s_sb[:, f, :],
                                                  start=(f == 0), stop=(f == F0 - 1))
                        if f == F0 - 1:
                            mm.then_inc(out2_done, 1)
                    if k == PER_BT and h == H1_AT:
                        pe.wait_ge(out2_ready, t + 1)
                        pe.wait_ge(sum0_done, 4 * t + 4)
                        if exists(t, k + 2):
                            pe.wait_ge(x0t_ready, 4 * t + k + 3)
                        for m in range(H1 // 128):
                            cols = slice(m * 128, (m + 1) * 128)
                            to = turn_ps[:, m * BT:(m + 1) * BT]
                            nc.tensor.matmul(to, wt1_sb[:, 0, cols], out0[:, :], start=True, stop=False)
                            nc.tensor.matmul(to, wt1_sb[:, 1, cols], s_sb[:, F0, :], start=False, stop=False)
                            nc.tensor.matmul(to, wt1_sb[:, 2, cols], out2[:, :], start=False, stop=False)
                            mm = nc.tensor.matmul(to, wt1d_sb[:, cols], dense_sb[:, bass.ds(t * BT, BT)],
                                                  start=False, stop=True)
                        mm.then_inc(h1_done, 1)
                    if k == PER_BT and h == H2_AT:
                        pe.wait_ge(h1_ready, t + 1)
                        for m in range(H2 // 128):
                            for q in range(H1 // 128):
                                mm = nc.tensor.matmul(s_ps[:, m * BT:(m + 1) * BT], wt2_sb[:, q, m * 128:(m + 1) * 128],
                                                      h1_sb[:, q, :], start=(q == 0), stop=(q == H1 // 128 - 1))
                        mm.then_inc(h2_done, 1)
                    if k == PER_BT and h == Y_AT:
                        pe.wait_ge(h2_ready, t + 1)
                        for q in range(H2 // 128):
                            mm = nc.tensor.matmul(turn_ps[0:1, 0:BT], wt3_sb[:, q:q + 1], h2_sb[:, q, :],
                                                  start=(q == 0), stop=(q == H2 // 128 - 1))
                        mm.then_inc(y_done, 1)
                    if exists(t, k):
                        n = HALVES * k + h
                        if n == 0 and isinstance(t, int) and t == 0:
                            pe.wait_ge(w1_lo_ready, 1)
                        wait_z_lo(pe, t, n)
                        rows = FG_ROWS[i]
                        for jj in range(2):
                            w = GG * i + 2 * (h % 2) + jj
                            acc = x2_ps[k % 2][:, :]
                            hi, lo = z_hi[0:rows, n % RING, jj, :], z_lo[0:rows, n % RING, jj, :]
                            nc.tensor.matmul(acc, w1_hi[0:rows, w, :], hi, start=(w == 0), stop=False)
                            nc.tensor.matmul(acc, w1_hi[0:rows, w, :], lo, start=False, stop=False)
                            mm = nc.tensor.matmul(acc, w1_lo[0:rows, w, :], hi, start=False,
                                                  stop=(w == FG * GG - 1))
                        mm.then_inc(l1_done, 1)
                    if h in S_AT and exists(t, k - 1):
                        s = S_AT.index(h)
                        pe.wait_ge(diag_ready, SUBS * 4 * t + SUBS * (k - 1) + s + 1)
                        if s > 0:
                            pe.wait_ge(s_ready, SUBS * 4 * t + SUBS * (k - 1) + s)
                        nc.tensor.matmul(s_ps[:, 0:SB * (F0 + 1)], x2t_sb[:, s % 2, 0:128],
                                         diag_sb[:, s % 2, :, :].rearrange("p b f -> p (b f)"),
                                         start=True, stop=True).then_inc(s_done, 1)

            def first_pairs():
                def select(i):
                    if i >= 4:
                        pe.wait_ge(z0_ready, i - 3)
                    nc.tensor.matmul(first_banks[i % 4][0:T0_ROWS[i], :],
                                     sel_sb[0:XR, SEL_B + 3 * F0 * i:SEL_B + 3 * F0 * i + T0_ROWS[i]],
                                     x0t[:, 0, :], start=True, stop=True).then_inc(pair_done, 1)

                pe.wait_ge(a_ready, 1)
                for i in range(4):
                    select(i)
                pe.wait_ge(w0_ready, 1)
                for i, rows in enumerate(T0_ROWS):
                    pe.wait_ge(z0_ready, i + 1)
                    mm = nc.tensor.matmul(x1_ps[:, :], w0_sb[0:rows, i, :], z_sb[0:rows, i // 2, i % 2, :],
                                          start=(i == 0), stop=(i == T0 - 1))
                    if i + 4 < T0:
                        select(i + 4)
                mm.then_inc(x1_done, 1)

            slots(pe, slot, first_pairs)


def constants():
    import numpy as np
    one = 0x3F80
    sel = np.zeros((128, SEL_COLS), np.uint16)
    f = np.arange(F0)
    for part in range(PARTS):
        rows = part * F0 + f
        for s in range(3):
            sel[rows, SEL_A + s * F0 + f] = one
        for s in range(SHIFTS):
            sel[part * F0 + (f + s) % F0, SEL_B + s * F0 + f] = one
        for field in range(F0):
            sel[part * F0 + field, SEL_F + 32 * field:SEL_F + 32 * (field + 1)] = one
        sel[rows, SEL_3 + f] = one
    sel[np.arange(128), IDB + np.arange(128)] = one
    eye_mask = np.zeros((128, 128 + SB), np.float32)
    eye_mask[np.arange(128), np.arange(128)] = 1
    eye_mask[np.arange(128), 128 + np.arange(128) % SB] = 1
    return sel, eye_mask


def kernel(dense_ctx, ids, W_top1, b_top1, W_top2, b_top2, W_top3, L0_rec_f0, L0_rec_f1, L0_rec_f2, **tables):
    import numpy as np
    import concourse.bacc as bacc
    from concourse.bass_utils import run_bass_kernel_spmd

    sel, eye_mask = constants()
    f = np.arange(F0)

    def pair_rows(w, mirrored):
        out = np.zeros((3 * F0, T0, MAPS), np.float32)
        for s in range(1 if mirrored else 0, SHIFTS):
            g = (f + s) % F0
            out[s % 3 * F0 + f, s // 3] = w[g * F0 + f if mirrored else f * F0 + g]
        return out

    f0, f1, f2 = (np.asarray(a) for a in (L0_rec_f0, L0_rec_f1, L0_rec_f2))
    padded = np.zeros((4 * FG, MAPS, MAPS), np.float32)
    padded[0:F0] = f1.reshape(F0, MAPS, MAPS)
    arrays = {
        "dense_t": np.asarray(dense_ctx).T,
        "ids_in": np.asarray(ids).reshape(B // BT, BT, F0).transpose(1, 0, 2),
        "w0a": pair_rows(f0, False),
        "w0b": pair_rows(f0, True),
        "w1": padded.reshape(FG, 4, GG, 32, MAPS).transpose(1, 3, 0, 2, 4).reshape(128, FG * GG, MAPS),
        "w2": f2.reshape(F0, MAPS, MAPS).transpose(1, 0, 2),
        "wt1": np.asarray(W_top1)[0:3 * MAPS].reshape(3, MAPS, H1).transpose(1, 0, 2),
        "wt1d": np.asarray(W_top1)[3 * MAPS:],
        "wt2": np.asarray(W_top2).reshape(H1 // 128, 128, H2).transpose(1, 0, 2),
        "wt3": np.asarray(W_top3).reshape(H2 // 128, 128).T,
        "bt1": np.asarray(b_top1).reshape(H1 // 128, 128).T,
        "bt2": np.asarray(b_top2).reshape(H2 // 128, 128).T,
        "sel": sel,
        "eye_mask": eye_mask,
    }
    for i in range(F0):
        arrays[f"tbl_{i}"] = np.asarray(tables[f"tbl_{i}"])
    arrays = {"in_" + n: np.ascontiguousarray(a) for n, a in arrays.items()}

    nc = bacc.Bacc("TRN2", target_bir_lowering=False, num_devices=1)
    a = {n: nc.dram_tensor(n, x.shape, mybir.dt.from_np(x.dtype), kind="ExternalInput").ap() for n, x in arrays.items()}
    y = nc.dram_tensor("out_y", (1, B), mybir.dt.float32, kind="ExternalOutput").ap()
    dlrm_tower(nc, a["in_dense_t"], a["in_ids_in"], [a[f"in_tbl_{i}"] for i in range(F0)], a["in_w0a"], a["in_w0b"],
               a["in_w1"], a["in_w2"], a["in_wt1"], a["in_wt1d"], a["in_wt2"], a["in_wt3"], a["in_bt1"], a["in_bt2"],
               a["in_sel"], a["in_eye_mask"], y)
    r = run_bass_kernel_spmd(nc, [arrays], core_ids=[0])
    return r.results[0]["out_y"].reshape(B, 1)
```

```python
import concourse.bass as bass
from concourse import mybir
from contextlib import ExitStack

F0, D, MAPS = 39, 16, 128
B, CB, SB = 512, 32, 8
CHUNKS = B // CB
COLS = CB * D
SUBS = CB // SB
BT, PER_BT = 128, 128 // CB
PAIR, PAIRS = 2 * CB, B // (2 * CB)
PARTS = 3
FQ, XQ = (F0 + 3) // 4, 32
FH, XH = 2 * FQ, 2 * XQ
SHIFTS = (F0 + 1) // 2
T0 = (SHIFTS + 2) // 3
T0_ROWS = [min(3, SHIFTS - 3 * t) * F0 for t in range(T0)]
FG = (F0 + 3) // 4
FG_ROWS = [32 * min(4, F0 - 4 * i) for i in range(FG)]
GG = MAPS // 32
HALVES = 2 * FG
RING = 4
H1, H2 = 512, 256
POOL_LO = [(1, 3, 6, 8, 9, 10, 11, 12, 14, 15, 17, 18, 19), (0, 1, 3, 5, 8, 9, 10, 12, 16, 18),
           (2, 3, 6, 8, 9, 11, 12, 14, 15, 17, 18, 19), (1, 3, 4, 6, 7, 9, 11, 14, 18)]
LAST_POOL_LO = [(3, 5, 7, 8, 10, 11, 13, 14, 16, 18), (0, 2, 4, 5, 7, 8, 10, 11, 13, 14, 16, 18),
                (0, 2, 3, 5, 7, 8, 10, 11, 13, 14, 16)]
LAST_FROM = 4
GATHER_STEPS = 24
AHEAD_Z, AHEAD_POOL, AHEAD_DVE = 3, 2, 1
PAIR_AT = (0, 2, 4, 5, 6, 8, 10)
X1_AT = (1, 3, 5, 6, 7, 9, 11)
OUT2_AT, H1_AT, H2_AT, Y_AT = range(12, 23), 24, 26, 35
SUM0_AT = 5
S_START = (2, 6, 3, 8)
SPLIT_AT = (6, 9, 11, 13)
X0_TURN_AT = (14, 16)

SEL_A = 0
SEL_B = SEL_A + 3 * F0
SEL_F = SEL_B + T0 * 3 * F0
SEL_3 = SEL_F + FG * 128
IDB = SEL_3 + F0 + 1
SEL_COLS = IDB + 128


def s_at(k):
    return [[S_START[k % PER_BT] + i + 2 * s for s in range(SUBS)] for i in range(4)]


def dlrm_tower(nc, dense_t, ids, table_rows, first_ids, first_table_rows, tables, w0a, w0b, w1, w2, wt1, wt1d,
               wt2, wt3, bt1, bt2, sel, eye_mask, x1_dram, y):
    fp32, bf16, f32r, i32 = mybir.dt.float32, mybir.dt.bfloat16, mybir.dt.float32r, mybir.dt.int32
    ALU, ACT, AX = mybir.AluOpType, mybir.ActivationFunctionType, mybir.AxisListType

    with ExitStack() as ctx:
        def sb(name, shape, dt=fp32):
            return ctx.enter_context(nc.sbuf_tensor(name, shape, dt))

        def bank(name):
            return ctx.enter_context(nc.psum_tensor(name, [128, 512], fp32))

        def sem(name):
            return ctx.enter_context(nc.semaphore(name))

        sel_sb = sb("sel_sb", [128, SEL_COLS], bf16)
        sel_a = sel_sb[:, SEL_A:SEL_A + 3 * F0]
        eye_sb = sb("eye_sb", [128, 128 + SB])
        eye = eye_sb[:, 0:128]
        mask = eye_sb[:, 128:128 + SB]
        spread_sel = sb("spread_sel", [128, GG, 128])
        w0_sb = sb("w0_sb", [3 * F0, T0, MAPS])
        w1_hi = sb("w1_hi", [128, FG * GG, MAPS], f32r)
        w1_lo = sb("w1_lo", [128, FG * GG, MAPS], f32r)
        w2_sb = sb("w2_sb", [128, F0, MAPS])
        wt1_sb = sb("wt1_sb", [128, 3, H1])
        wt1d_sb = sb("wt1d_sb", [D, H1])
        wt2_sb = sb("wt2_sb", [128, H1 // 128, H2])
        wt3_sb = sb("wt3_sb", [128, H2 // 128])
        bt1_sb = sb("bt1_sb", [128, H1 // 128])
        bt2_sb = sb("bt2_sb", [128, H2 // 128])
        dense_sb = sb("dense_sb", [D, B])
        ids_sb = sb("ids_sb", [128, PAIRS, FH], i32)
        table_rows_sb = sb("table_rows_sb", [128, 1, FH], i32)
        ids_now = sb("ids_now", [128, 1, FH], i32)
        first_ids_sb = sb("first_ids_sb", [128, 2, FQ], i32)
        first_table_rows_sb = sb("first_table_rows_sb", [128, 1, FQ], i32)
        e_first = sb("e_first", [128, 2, FQ, D])
        e_sb = sb("e_sb", [128, FH, D])
        e_rest = sb("e_rest", [128, D, FH])
        e_parts = sb("e_parts", [128, D, XH], bf16)
        x0t = sb("x0t", [128, 4, COLS], bf16)
        a_sb = sb("a_sb", [3 * F0, COLS])
        z0_sb = sb("z0_sb", [3 * F0, COLS])
        x1_sb = sb("x1_sb", [128, 2, COLS])
        x1_rep = sb("x1_rep", [128, 2, GG, COLS])
        z_sb = sb("z_sb", [128, RING, 2, COLS])
        z_hi = sb("z_hi", [128, RING, 2, COLS], f32r)
        z_lo = sb("z_lo", [128, RING, 2, COLS], f32r)
        x2_sb = sb("x2_sb", [128, COLS])
        x2t_sb = sb("x2t_sb", [128, 2, 128 + F0 + 1])
        diag_sb = sb("diag_sb", [128, 2, SB, F0 + 1])
        s_sb = sb("s_sb", [128, FG * GG, BT])
        out0 = sb("out0", [128, BT])
        out2 = sb("out2", [128, BT])
        h1_sb = sb("h1_sb", [128, H1 // 128, BT])
        h2_sb = sb("h2_sb", [128, H2 // 128, BT])
        y_sb = sb("y_sb", [1, B])
        w0_raw = z_sb[0:3 * F0, :, :, :].rearrange("p r j c -> p (r j c)")
        w0a_raw = w0_raw[:, 0:T0 * MAPS].rearrange("p (t m) -> p t m", t=T0)
        w0b_raw = w0_raw[:, T0 * MAPS:2 * T0 * MAPS].rearrange("p (t m) -> p t m", t=T0)

        rep_ps = [bank("rep_ps0"), bank("rep_ps1")]
        pair_ps = bank("pair_ps")
        x1_ps = bank("x1_ps")
        x2_ps = [bank("x2_ps0"), bank("x2_ps1")]
        turn_ps = bank("turn_ps")
        s_ps = bank("s_ps")
        first_banks = [pair_ps, s_ps, x2_ps[0], x2_ps[1]]

        consts_in = sem("consts_in")
        first_ids_in = sem("first_ids_in")
        ids_in = sem("ids_in")
        w0_in = sem("w0_in")
        w1_in = sem("w1_in")
        late_in = sem("late_in")
        first_ids_moved = sem("first_ids_moved")
        first_in = [sem("first_in0"), sem("first_in1")]
        first_step = sem("first_step")
        first_split = sem("first_split")
        ids_moved = sem("ids_moved")
        e_in = sem("e_in")
        e_step = sem("e_step")
        e_split = sem("e_split")
        turned = sem("turned")
        x0t_ready = sem("x0t_ready")
        spread_sel_ready = sem("spread_sel_ready")
        w0_ready = sem("w0_ready")
        w1_hi_ready = sem("w1_hi_ready")
        w1_lo_ready = sem("w1_lo_ready")
        pads_ready = sem("pads_ready")
        a_done = sem("a_done")
        a_ready = sem("a_ready")
        pair_done = sem("pair_done")
        z0_ready = sem("z0_ready")
        x1_done = sem("x1_done")
        x1_ready = sem("x1_ready")
        x1_stored = sem("x1_stored")
        x1_spread = [[sem(f"x1_spread{p}{jp}") for jp in range(2)] for p in range(2)]
        first_spread_done = sem("first_spread_done")
        first_spread = sem("first_spread")
        rep_done = sem("rep_done")
        z_ready = sem("z_ready")
        z_hi_ready = sem("z_hi_ready")
        z_lo_pool = sem("z_lo_pool")
        z_lo_dve = sem("z_lo_dve")
        l1_done = sem("l1_done")
        x2_ready = sem("x2_ready")
        sum0_done = sem("sum0_done")
        x2t_done = sem("x2t_done")
        x2t_ready = sem("x2t_ready")
        diag_ready = sem("diag_ready")
        s_done = sem("s_done")
        s_ready = sem("s_ready")
        out2_done = sem("out2_done")
        out2_ready = sem("out2_ready")
        h1_done = sem("h1_done")
        h1_ready = sem("h1_ready")
        h2_done = sem("h2_done")
        h2_ready = sem("h2_ready")
        y_done = sem("y_done")
        y_ready = sem("y_ready")
        y_stored = sem("y_stored")

        def on_pool(t, n):
            last = HALVES * (CHUNKS - len(LAST_POOL_LO))
            if isinstance(t, int) and HALVES * 4 * t + n >= last + LAST_FROM:
                n = HALVES * 4 * t + n - last
                return n % HALVES in LAST_POOL_LO[n // HALVES]
            return n % HALVES in POOL_LO[n // HALVES % PER_BT]

        per_tile = {pool_has: sum(on_pool(0, n) == pool_has for n in range(HALVES * PER_BT)) for pool_has in (True, False)}

        def wait_z_lo(eng, t, n):
            mine = on_pool(t, n)
            if isinstance(t, int):
                count = sum(on_pool(0, i) == mine for i in range(HALVES * 4 * t + n + 1))
            else:
                whole = n // (HALVES * PER_BT)
                count = per_tile[mine] * (t + whole) + \
                    sum(on_pool(0, i) == mine for i in range(n - whole * HALVES * PER_BT + 1))
            eng.wait_ge(z_lo_pool if mine else z_lo_dve, count)

        def parts_of(e, part):
            return e[:, :, :].rearrange("p d (u r) -> p d u r", u=2)[:, :, :, FQ * part:min(FQ * (part + 1), XQ)]

        LATE = 8
        SPREADS = 16 * 2

        def exists(t, k):
            return not isinstance(t, int) or 0 <= 4 * t + k < CHUNKS

        def slots(eng, one, first=None):
            one(0, -2)
            if first:
                first()
            for k in range(-1, PER_BT + 1):
                one(0, k)
            with eng.Fori(1, B // BT - 1) as t:
                for k in range(1, PER_BT + 1):
                    one(t, k)
            for k in range(1, PER_BT + 1):
                one(B // BT - 1, k)
            one(B // BT, 1)

        def mlp_step(t, k, h):
            if k == PER_BT:
                return t, h
            if k == 1 and (not isinstance(t, int) or t > 0):
                return t - 1, HALVES + h
            return None, None

        block = ctx.enter_context(nc.Block())

        @block.sync
        def _(sp):
            sp.dma_start(first_ids_sb[:, :, :], first_ids).then_inc(first_ids_in, 16)
            sp.dma_start(first_table_rows_sb[:, :, :], first_table_rows).then_inc(first_ids_in, 16)
            sp.dma_start(ids_sb[:, :, :], ids).then_inc(ids_in, 16)
            sp.dma_start(table_rows_sb[:, :, :], table_rows).then_inc(ids_in, 16)
            sp.dma_start(sel_sb[:, :], sel.bitcast(bf16)).then_inc(consts_in, 16)
            sp.dma_start(eye_sb[:, :], eye_mask).then_inc(consts_in, 16)
            sp.dma_start(w0a_raw, w0a).then_inc(w0_in, 16)
            sp.dma_start(w0b_raw, w0b).then_inc(w0_in, 16)
            sp.wait_ge(first_in[0], 16 * FQ)
            sp.dma_start(s_sb[:, :, :], w1).then_inc(w1_in, 16)
            sp.wait_ge(first_in[1], 16 * FQ)
            sp.dma_start(w2_sb[:, :, :], w2).then_inc(late_in, 16)
            sp.dma_start(wt1_sb[:, :, :], wt1).then_inc(late_in, 16)
            sp.dma_start(wt1d_sb[:, :], wt1d).then_inc(late_in, 16)
            sp.dma_start(wt2_sb[:, :, :], wt2).then_inc(late_in, 16)
            sp.dma_start(wt3_sb[:, :], wt3).then_inc(late_in, 16)
            sp.dma_start(bt1_sb[:, :], bt1).then_inc(late_in, 16)
            sp.dma_start(bt2_sb[:, :], bt2).then_inc(late_in, 16)
            sp.dma_start(dense_sb[:, :], dense_t).then_inc(late_in, 16)

            def slot(t, k):
                n = k + 1
                if exists(t, n) and k != -1:
                    sp.wait_ge(x1_ready, 4 * t + n + 1)
                    sp.dma_start(x1_dram[n % 2], x1_sb[:, n % 2, :]).then_inc(x1_stored, 16)
                    sp.wait_ge(x1_stored, 16 * 4 * t + 16 * n)
                    for j in range(GG):
                        group = x1_dram[n % 2, 32 * j:32 * j + 32, :].rearrange("(a m) c -> a m c", a=1)
                        sp.dma_start(x1_rep[:, n % 2, j, :], group.broadcast_to([4, 32, COLS]))\
                            .then_inc(x1_spread[n % 2][j // 2], 16)

            slots(sp, slot)
            sp.wait_ge(y_ready, B // BT)
            sp.dma_start(y, y_sb[:, :]).then_inc(y_stored, 16)
            sp.wait_ge(y_stored, 16)

        @block.gpsimd
        def _(pool):
            nc.gpsimd.memset(e_sb[:, FH - 1, :], 0.0).then_inc(pads_ready, 1)
            nc.gpsimd.memset(e_first[:, :, FQ - 1, :], 0.0).then_inc(pads_ready, 1)
            nc.gpsimd.memset(parts_of(e_parts, PARTS), 0.0).then_inc(pads_ready, 1)
            for half in range(2):
                nc.gpsimd.memset(x2t_sb[:, half, 128 + F0:], 1.0).then_inc(pads_ready, 1)

            pool.wait_ge(first_ids_in, 32)
            nc.gpsimd.tensor_tensor(first_ids_sb[:, :, :], first_ids_sb[:, :, :],
                                    first_table_rows_sb[:, :, :].broadcast_to([128, 2, FQ]),
                                    ALU.add).then_inc(first_ids_moved, 1)
            pool.wait_ge(pads_ready, 5)
            pool.wait_ge(first_ids_moved, 1)
            for n in range(2):
                for i in range(FQ):
                    rows = 128 if 3 * FQ + i < F0 else 3 * XQ
                    pool.indirect_dma_start(
                        out=e_first[0:rows, n, i, :], out_offset=None, in_=tables,
                        in_offset=bass.IndirectOffsetOnAxis(ap=first_ids_sb[0:rows, n, i:i + 1], axis=0))\
                        .then_inc(first_in[n], 16)
            pool.wait_ge(ids_in, 32)

            def gather(pair, step):
                if step == 0:
                    if not isinstance(pair, int) or pair > 1:
                        pool.wait_ge(e_split, pair - 1)
                    nc.gpsimd.tensor_tensor(ids_now[:, :, :], ids_sb[:, bass.ds(pair, 1), :],
                                            table_rows_sb[:, :, :], ALU.add).then_inc(ids_moved, 1)
                    return
                for i in range(FH * (step - 1) // (GATHER_STEPS - 1), FH * step // (GATHER_STEPS - 1)):
                    rows = 128 if FH + i < F0 else XH
                    pool.indirect_dma_start(
                        out=e_sb[0:rows, i, :], out_offset=None, in_=tables,
                        in_offset=bass.IndirectOffsetOnAxis(ap=ids_now[0:rows, 0, i:i + 1], axis=0)).then_inc(e_in, 16)

            def slot(t, k):
                turn_at, turned_at, diag_at, copy_at = s_at(k)
                for h in range(HALVES):
                    tile, step = mlp_step(t, k, h)
                    if k % 2 == 1 and h == 1 and exists(t, k + 3):
                        pool.wait_ge(ids_moved, 2 * t + (k + 3) // 2)
                    if h in diag_at and exists(t, k - 1):
                        s = diag_at.index(h)
                        pool.wait_ge(x2t_ready, SUBS * 4 * t + SUBS * (k - 1) + s + 1)
                        nc.gpsimd.tensor_tensor(
                            diag_sb[:, s % 2, :, :],
                            x2t_sb[:, s % 2, 128:].rearrange("p (a f) -> p a f", a=1).broadcast_to([128, SB, F0 + 1]),
                            mask.rearrange("p (b a) -> p b a", a=1).broadcast_to([128, SB, F0 + 1]),
                            ALU.mult).then_inc(diag_ready, 1)
                    n = HALVES * k + h + AHEAD_POOL
                    if exists(t, k + (h + AHEAD_POOL) // HALVES) and on_pool(t, n):
                        pool.wait_ge(z_hi_ready, HALVES * 4 * t + n + 1)
                        if not isinstance(t, int) or HALVES * 4 * t + n >= RING:
                            pool.wait_ge(l1_done, HALVES * 4 * t + n + 1 - RING)
                        nc.gpsimd.tensor_tensor(z_lo[:, n % RING, :, :], z_sb[:, n % RING, :, :],
                                                z_hi[:, n % RING, :, :].bitcast(fp32),
                                                ALU.subtract).then_inc(z_lo_pool, 1)
                    if k % 2 == 1 and exists(t, k + 3):
                        gather(2 * t + (k + 3) // 2, h)
                    if k % 2 == 0 and k > -2 and h < GATHER_STEPS - HALVES and exists(t, k + 2):
                        gather(2 * t + (k + 2) // 2, HALVES + h)

            slots(pool, slot)

        @block.scalar
        def _(act):
            def round_w1():
                act.wait_ge(w1_in, 16)
                nc.scalar.activation(w1_hi[:, :, :], s_sb[:, :, :], ACT.Copy).then_inc(w1_hi_ready, 1)

            def first_turned(n):
                act.wait_ge(turned, n + 1)
                nc.scalar.activation(x0t[:, n, :].rearrange("p (s d b) -> p d s b", s=SUBS, d=D),
                                     turn_ps[:, :].rearrange("p (d s b) -> p d s b", d=D, s=SUBS),
                                     ACT.Copy).then_inc(x0t_ready, 1)

            first_turned(0)

            def slot(t, k):
                turn_at, turned_at, diag_at, copy_at = s_at(k)
                for h in range(HALVES):
                    tile, step = mlp_step(t, k, h)
                    if h == 0 and exists(t, k - 1):
                        act.wait_ge(l1_done, HALVES * 4 * t + HALVES * k)
                        nc.scalar.activation(x2_sb[:, :], x2_ps[(k - 1) % 2][:, :], ACT.Copy).then_inc(x2_ready, 1)
                    if h in turned_at and exists(t, k - 1):
                        s = turned_at.index(h)
                        act.wait_ge(x2t_done, SUBS * 4 * t + SUBS * (k - 1) + s + 1)
                        nc.scalar.activation(x2t_sb[:, s % 2, 0:128 + F0], turn_ps[:, 0:128 + F0], ACT.Copy)\
                            .then_inc(x2t_ready, 1)
                    if h in copy_at and exists(t, k - 1):
                        s = copy_at.index(h)
                        act.wait_ge(s_done, SUBS * 4 * t + SUBS * (k - 1) + s + 1)
                        at = (k - 1) % PER_BT * CB + s * SB
                        nc.scalar.activation(s_sb[:, 0:F0 + 1, at:at + SB].rearrange("p f b -> p b f"),
                                             s_ps[:, 0:SB * (F0 + 1)].rearrange("p (b f) -> p b f", b=SB),
                                             ACT.Copy).then_inc(s_ready, 1)
                    if h == X1_AT[-1] and exists(t, k + 1):
                        act.wait_ge(x1_done, 4 * t + k + 2)
                        if not isinstance(t, int) or 4 * t + k + 1 >= 2:
                            if not isinstance(t, int) or 4 * t + k + 1 > 2:
                                act.wait_ge(x1_stored, 16 * 4 * t + 16 * (k - 1))
                            act.wait_ge(sum0_done, 4 * t + k)
                        nc.scalar.activation(x1_sb[:, (k + 1) % 2, :], x1_ps[:, :], ACT.Copy).then_inc(x1_ready, 1)
                    if k == -1 and h == HALVES - AHEAD_Z - 1:
                        for j in range(GG):
                            act.wait_ge(first_spread_done, j + 1)
                            nc.scalar.activation(x1_rep[:, 0, j, :], first_banks[j][:, :],
                                                 ACT.Copy).then_inc(first_spread, 1)
                    if k % 2 == 0 and k > -2 and h - 1 in X0_TURN_AT and exists(t, k + 2):
                        part = X0_TURN_AT.index(h - 1)
                        act.wait_ge(turned, 4 * t + k + 2 + part + 1)
                        for q in range(2):
                            last = nc.scalar.activation(
                                x0t[:, (k + 2 + q) % 4, :].rearrange("p (s d b) -> p d s b", s=SUBS, d=D)
                                [:, D // 2 * part:D // 2 * (part + 1), :, :],
                                turn_ps[:, :].rearrange("p (d q s b) -> p d q s b", d=D // 2, q=2, s=SUBS)
                                [:, :, q, :, :], ACT.Copy)
                        last.then_inc(x0t_ready, 1)
                    if h == HALVES - 1 and k == -1:
                        first_turned(1)
                    if h == HALVES - 1 and exists(t, k + 2):
                        act.wait_ge(a_done, 4 * t + k + 3)
                        nc.scalar.activation(a_sb[:, :], pair_ps[0:3 * F0, :], ACT.Copy).then_inc(a_ready, 1)
                    if step == OUT2_AT[-1] + 1:
                        act.wait_ge(out2_done, tile + 1)
                        nc.scalar.activation(out2[:, :], s_ps[:, 0:BT], ACT.Copy).then_inc(out2_ready, 1)
                    if step == H1_AT + 1:
                        act.wait_ge(late_in, 16 * LATE)
                        act.wait_ge(h1_done, tile + 1)
                        for m in range(H1 // 128):
                            last = nc.scalar.activation(h1_sb[:, m, :], turn_ps[:, m * BT:(m + 1) * BT], ACT.Relu,
                                                        bias=bt1_sb[:, m:m + 1])
                        last.then_inc(h1_ready, 1)
                    if step == H2_AT + 1:
                        act.wait_ge(h2_done, tile + 1)
                        for m in range(H2 // 128):
                            last = nc.scalar.activation(h2_sb[:, m, :], s_ps[:, m * BT:(m + 1) * BT], ACT.Relu,
                                                        bias=bt2_sb[:, m:m + 1])
                        last.then_inc(h2_ready, 1)
                    if step == Y_AT + 1:
                        act.wait_ge(y_done, tile + 1)
                        row = tile * BT if isinstance(t, int) else act.snap(tile * BT)
                        nc.scalar.activation(y_sb[:, bass.ds(row, BT)], turn_ps[0:1, 0:BT],
                                             ACT.Copy).then_inc(y_ready, 1)
                    n = HALVES * k + h + AHEAD_Z
                    if exists(t, k + (h + AHEAD_Z) // HALVES):
                        act.wait_ge(z_ready, HALVES * 4 * t + n + 1)
                        if not isinstance(t, int) or HALVES * 4 * t + n >= RING:
                            act.wait_ge(l1_done, HALVES * 4 * t + n + 1 - RING)
                        nc.scalar.activation(z_hi[:, n % RING, :, :], z_sb[:, n % RING, :, :],
                                             ACT.Copy).then_inc(z_hi_ready, 1)

            slots(act, slot, round_w1)

        @block.vector
        def _(dve):
            dve.wait_ge(consts_in, 32)
            nc.vector.tensor_copy(
                spread_sel[:, :, :].rearrange("p j (r m) -> p j r m", r=4),
                eye.rearrange("p (j a m) -> p j a m", j=GG, a=1).broadcast_to([128, GG, 4, 32])).then_inc(spread_sel_ready, 1)
            dve.wait_ge(w0_in, 32)
            nc.vector.tensor_tensor(w0_sb[:, :, :], w0a_raw, w0b_raw, ALU.add).then_inc(w0_ready, 1)

            def split(step, whole, rest, part, step_done, before, split_done):
                if step == 0:
                    nc.vector.tensor_copy(part(0), whole).then_inc(step_done, 1)
                    dve.wait_ge(step_done, before + 1)
                if step == 1:
                    nc.vector.tensor_tensor(rest, whole, part(0), ALU.subtract).then_inc(step_done, 1)
                    dve.wait_ge(step_done, before + 2)
                if step == 2:
                    nc.vector.tensor_copy(part(1), rest).then_inc(step_done, 1)
                    dve.wait_ge(step_done, before + 3)
                if step == 3:
                    nc.vector.tensor_tensor(part(2), rest, part(1), ALU.subtract).then_inc(split_done, 1)

            def split_first(n):
                dve.wait_ge(first_in[n], 16 * FQ)
                for step in range(4):
                    split(step, e_first[:, n, :, :].rearrange("p i d -> p d i"), e_rest[:, :, FQ * n:FQ * (n + 1)],
                          lambda part: parts_of(e_parts, part)[:, :, n, :], first_step, 3 * n, first_split)

            def split_pair(pair, step):
                if step == 0:
                    dve.wait_ge(e_in, 16 * FH * pair)
                    dve.wait_ge(turned, 2 * pair)
                split(step, e_sb[:, :, :].rearrange("p (u i) d -> p d u i", u=2),
                      e_rest[:, :, :].rearrange("p d (u i) -> p d u i", u=2),
                      lambda part: parts_of(e_parts, part), e_step, 3 * (pair - 1), e_split)

            dve.wait_ge(pads_ready, 5)
            split_first(0)

            def slot(t, k):
                turn_at, turned_at, diag_at, copy_at = s_at(k)
                for h in range(HALVES):
                    tile, step = mlp_step(t, k, h)
                    if exists(t, k + (h + AHEAD_Z) // HALVES):
                        n = HALVES * k + h + AHEAD_Z
                        i, jp = n % HALVES // 2, n % 2
                        dve.wait_ge(rep_done, FG * 4 * t + n // 2 + 1)
                        at = k + 1
                        if n < 2:
                            dve.wait_ge(first_spread, 2 * jp + 2)
                        elif n % HALVES < 2:
                            dve.wait_ge(x1_spread[at % 2][jp], SPREADS * (2 * t) + SPREADS * ((at + 1) // 2))
                        if not isinstance(t, int) or HALVES * 4 * t + n >= RING:
                            dve.wait_ge(z_hi_ready, HALVES * 4 * t + n + 1 - RING)
                            wait_z_lo(dve, t, n - RING)
                        nc.vector.tensor_tensor(
                            z_sb[:, n % RING, :, :],
                            rep_ps[n // 2 % 2][:, :].rearrange("p (a c) -> p a c", a=1).broadcast_to([128, 2, COLS]),
                            x1_rep[:, n // HALVES % 2, 2 * jp:2 * jp + 2, :],
                            ALU.mult).then_inc(z_ready, 1)
                    if h in PAIR_AT and k != -1 and exists(t, k + 1):
                        i = PAIR_AT.index(h)
                        rows = T0_ROWS[i]
                        dve.wait_ge(pair_done, T0 * 4 * t + T0 * (k + 1) + i + 1)
                        nc.vector.tensor_tensor(z0_sb[0:rows, :], pair_ps[0:rows, :], a_sb[0:rows, :],
                                                ALU.mult).then_inc(z0_ready, 1)
                    n = HALVES * k + h + AHEAD_DVE
                    if exists(t, k + (h + AHEAD_DVE) // HALVES) and not on_pool(t, n):
                        dve.wait_ge(z_hi_ready, HALVES * 4 * t + n + 1)
                        if not isinstance(t, int) or HALVES * 4 * t + n >= RING:
                            dve.wait_ge(l1_done, HALVES * 4 * t + n + 1 - RING)
                        nc.vector.tensor_tensor(z_lo[:, n % RING, :, :], z_sb[:, n % RING, :, :],
                                                z_hi[:, n % RING, :, :].bitcast(fp32),
                                                ALU.subtract).then_inc(z_lo_dve, 1)
                    if h == SUM0_AT and exists(t, k - 1):
                        if tile is not None and k == 1:
                            dve.wait_ge(h1_done, tile + 1)
                        at = (k - 1) % PER_BT * CB
                        dve.wait_ge(x1_ready, 4 * t + k)
                        nc.vector.tensor_reduce(
                            out0[:, at:at + CB].rearrange("p (s b) -> p s b", s=SUBS),
                            x1_sb[:, (k - 1) % 2, :].rearrange("p (s d b) -> p s b d", s=SUBS, d=D),
                            axis=AX.X, op=ALU.add).then_inc(sum0_done, 1)
                    if k % 2 == 0 and k > -2 and h in SPLIT_AT and exists(t, k + 2):
                        split_pair(2 * t + (k + 2) // 2, SPLIT_AT.index(h))

            def first_pairs():
                dve.wait_ge(w0_ready, 1)
                dve.wait_ge(a_ready, 1)
                for i, rows in enumerate(T0_ROWS):
                    dve.wait_ge(pair_done, i + 1)
                    nc.vector.tensor_tensor(z_sb[0:rows, i // 2, i % 2, :], first_banks[i % 4][0:rows, :],
                                            a_sb[0:rows, :], ALU.mult).then_inc(z0_ready, 1)
                split_first(1)
                dve.wait_ge(w1_hi_ready, 1)
                nc.vector.tensor_tensor(w1_lo[:, :, :], s_sb[:, :, :], w1_hi[:, :, :].bitcast(fp32),
                                        ALU.subtract).then_inc(w1_lo_ready, 1)

            slots(dve, slot, first_pairs)

        @block.tensor
        def _(pe):
            pe.wait_ge(consts_in, 32)

            def turn_first(n):
                pe.wait_ge(first_split, n + 1)
                if n > 0:
                    pe.wait_ge(x0t_ready, n)
                for d in range(D):
                    for q in range(4):
                        rows = slice(XQ * q, XQ * (q + 1))
                        mm = nc.tensor.matmul(turn_ps[rows, CB * d:CB * (d + 1)],
                                              e_parts[rows, d, XQ * n:XQ * (n + 1)],
                                              sel_sb[rows, IDB + XQ * q:IDB + XQ * (q + 1)], start=True, stop=True)
                mm.then_inc(turned, 1)

            turn_first(0)

            def x0t_events(t, k):
                return 1 if isinstance(t, int) and 4 * t + k == 0 else 4 * t + 2 * (k // 2 + 1)

            def wait_x0_turned(t, k):
                pairs = 2 * t + (k + 1) // 2 + 1
                pe.wait_ge(x0t_ready, 2 * (pairs if not isinstance(t, int) else min(pairs, PAIRS)))

            def slot(t, k):
                turn_at, turned_at, diag_at, copy_at = s_at(k)
                for h in range(HALVES):
                    tile, step = mlp_step(t, k, h)
                    i = h // 2
                    turns_x0 = k % 2 == 0 and k > -2 and h in X0_TURN_AT and exists(t, k + 2)
                    if turns_x0 and h == X0_TURN_AT[0]:
                        pe.wait_ge(e_split, 2 * t + (k + 2) // 2)
                        if exists(t, k - 1):
                            pe.wait_ge(x2t_ready, SUBS * 4 * t + SUBS * k)
                    if turns_x0 and h == X0_TURN_AT[1]:
                        pe.wait_ge(x0t_ready, 4 * t + k + 3)
                    if h % 2 == 0 and exists(t, k + (i + 2) // FG):
                        g = FG * k + i + 2
                        at = (k + (i + 2) // FG) % 4
                        f = (i + 2) % FG
                        if g % FG == 0:
                            pe.wait_ge(x0t_ready, x0t_events(t, k + 1))
                        if not isinstance(t, int) or FG * 4 * t + g >= 2:
                            pe.wait_ge(z_ready, HALVES * 4 * t + 2 * (g - 1))
                        nc.tensor.matmul(rep_ps[g % 2][:, :], sel_sb[:, SEL_F + 128 * f:SEL_F + 128 * (f + 1)],
                                         x0t[:, at, :], start=True, stop=True).then_inc(rep_done, 1)
                    if k == -1 and h == HALVES - 2:
                        pe.wait_ge(x1_ready, 1)
                        pe.wait_ge(spread_sel_ready, 1)
                        for j in range(GG):
                            nc.tensor.matmul(first_banks[j][:, :], spread_sel[:, j, :], x1_sb[:, 0, :],
                                             start=True, stop=True).then_inc(first_spread_done, 1)
                        turn_first(1)
                    if h in X1_AT and k != -1 and exists(t, k + 1):
                        q = X1_AT.index(h)
                        rows = T0_ROWS[q]
                        pe.wait_ge(z0_ready, T0 * 4 * t + T0 * (k + 1) + q + 1)
                        if q == 0:
                            pe.wait_ge(x1_ready, 4 * t + k + 1)
                        mm = nc.tensor.matmul(x1_ps[:, :], w0_sb[0:rows, q, :], z0_sb[0:rows, :],
                                              start=(q == 0), stop=(q == T0 - 1))
                        if q == T0 - 1:
                            mm.then_inc(x1_done, 1)
                    if h in PAIR_AT and k != -1 and exists(t, k + 1):
                        q = PAIR_AT.index(h)
                        rows = T0_ROWS[q]
                        if q == 0:
                            pe.wait_ge(a_ready, 4 * t + k + 2)
                        nc.tensor.matmul(pair_ps[0:rows, :],
                                         sel_sb[:, SEL_B + 3 * F0 * q:SEL_B + 3 * F0 * q + rows],
                                         x0t[:, (k + 1) % 4, :], start=True, stop=True).then_inc(pair_done, 1)
                    if h in turn_at and exists(t, k - 1):
                        s = turn_at.index(h)
                        if s == 0:
                            pe.wait_ge(x2_ready, 4 * t + k)
                            wait_x0_turned(t, k)
                            if tile is not None and k == 1:
                                pe.wait_ge(h1_ready, tile + 1)
                        else:
                            pe.wait_ge(x2t_ready, SUBS * 4 * t + SUBS * (k - 1) + s)
                        nc.tensor.transpose(turn_ps[:, 0:128], x2_sb[:, 128 * s:128 * s + 128], eye)
                        nc.tensor.matmul(turn_ps[:, 128:128 + F0], x0t[:, (k - 1) % 4, 128 * s:128 * s + 128],
                                         sel_sb[:, SEL_3:SEL_3 + F0], start=True, stop=True).then_inc(x2t_done, 1)
                    if turns_x0:
                        part = X0_TURN_AT.index(h)
                        for d in range(D // 2):
                            for half in range(2):
                                rows = slice(XH * half, XH * (half + 1))
                                mm = nc.tensor.matmul(turn_ps[rows, PAIR * d:PAIR * (d + 1)],
                                                      e_parts[rows, D // 2 * part + d, :],
                                                      sel_sb[rows, IDB + XH * half:IDB + XH * half + PAIR],
                                                      start=True, stop=True)
                        mm.then_inc(turned, 1)
                    if h == 19 and exists(t, k + 2):
                        pe.wait_ge(x0t_ready, x0t_events(t, k + 2))
                        if k == -1:
                            pe.wait_ge(first_spread, 1)
                        nc.tensor.matmul(pair_ps[0:3 * F0, :], sel_a, x0t[:, (k + 2) % 4, :],
                                         start=True, stop=True).then_inc(a_done, 1)
                    if step is not None and step in OUT2_AT:
                        q = OUT2_AT.index(step)
                        if q == 0:
                            pe.wait_ge(late_in, 16 * LATE)
                            pe.wait_ge(s_ready, SUBS * 4 * t + SUBS * PER_BT)
                        for f in range(F0 * q // len(OUT2_AT), F0 * (q + 1) // len(OUT2_AT)):
                            mm = nc.tensor.matmul(s_ps[:, 0:BT], w2_sb[:, f, :], s_sb[:, f, :],
                                                  start=(f == 0), stop=(f == F0 - 1))
                        if f == F0 - 1:
                            mm.then_inc(out2_done, 1)
                    if step == H1_AT:
                        pe.wait_ge(out2_ready, tile + 1)
                        pe.wait_ge(sum0_done, 4 * tile + 4)
                        wait_x0_turned(t, k)
                        for m in range(H1 // 128):
                            cols = slice(m * 128, (m + 1) * 128)
                            to = turn_ps[:, m * BT:(m + 1) * BT]
                            nc.tensor.matmul(to, wt1_sb[:, 0, cols], out0[:, :], start=True, stop=False)
                            nc.tensor.matmul(to, wt1_sb[:, 1, cols], s_sb[:, F0, :], start=False, stop=False)
                            nc.tensor.matmul(to, wt1_sb[:, 2, cols], out2[:, :], start=False, stop=False)
                            mm = nc.tensor.matmul(to, wt1d_sb[:, cols], dense_sb[:, bass.ds(tile * BT, BT)],
                                                  start=False, stop=True)
                        mm.then_inc(h1_done, 1)
                    if step == H2_AT:
                        pe.wait_ge(h1_ready, tile + 1)
                        for m in range(H2 // 128):
                            for q in range(H1 // 128):
                                mm = nc.tensor.matmul(s_ps[:, m * BT:(m + 1) * BT], wt2_sb[:, q, m * 128:(m + 1) * 128],
                                                      h1_sb[:, q, :], start=(q == 0), stop=(q == H1 // 128 - 1))
                        mm.then_inc(h2_done, 1)
                    if step == Y_AT:
                        pe.wait_ge(h2_ready, tile + 1)
                        if exists(t, k - 1):
                            pe.wait_ge(x2t_ready, SUBS * 4 * t + SUBS * k)
                        for q in range(H2 // 128):
                            mm = nc.tensor.matmul(turn_ps[0:1, 0:BT], wt3_sb[:, q:q + 1], h2_sb[:, q, :],
                                                  start=(q == 0), stop=(q == H2 // 128 - 1))
                        mm.then_inc(y_done, 1)
                    if exists(t, k):
                        n = HALVES * k + h
                        if n == 0 and isinstance(t, int) and t == 0:
                            pe.wait_ge(w1_lo_ready, 1)
                        wait_z_lo(pe, t, n)
                        rows = FG_ROWS[i]
                        for jj in range(2):
                            w = GG * i + 2 * (h % 2) + jj
                            acc = x2_ps[k % 2][:, :]
                            hi, lo = z_hi[0:rows, n % RING, jj, :], z_lo[0:rows, n % RING, jj, :]
                            nc.tensor.matmul(acc, w1_hi[0:rows, w, :], hi, start=(w == 0), stop=False)
                            nc.tensor.matmul(acc, w1_hi[0:rows, w, :], lo, start=False, stop=False)
                            mm = nc.tensor.matmul(acc, w1_lo[0:rows, w, :], hi, start=False,
                                                  stop=(w == FG * GG - 1))
                        mm.then_inc(l1_done, 1)
                    if h in diag_at and exists(t, k - 1):
                        s = diag_at.index(h)
                        if s == 0 and tile is not None and k == 1:
                            pe.wait_ge(h2_ready, tile + 1)
                        pe.wait_ge(diag_ready, SUBS * 4 * t + SUBS * (k - 1) + s + 1)
                        if s > 0:
                            pe.wait_ge(s_ready, SUBS * 4 * t + SUBS * (k - 1) + s)
                        nc.tensor.matmul(s_ps[:, 0:SB * (F0 + 1)], x2t_sb[:, s % 2, 0:128],
                                         diag_sb[:, s % 2, :, :].rearrange("p b f -> p (b f)"),
                                         start=True, stop=True).then_inc(s_done, 1)

            def first_pairs():
                def select(i):
                    if i >= 4:
                        pe.wait_ge(z0_ready, i - 3)
                    nc.tensor.matmul(first_banks[i % 4][0:T0_ROWS[i], :],
                                     sel_sb[:, SEL_B + 3 * F0 * i:SEL_B + 3 * F0 * i + T0_ROWS[i]],
                                     x0t[:, 0, :], start=True, stop=True).then_inc(pair_done, 1)

                pe.wait_ge(a_ready, 1)
                for i in range(4):
                    select(i)
                pe.wait_ge(w0_ready, 1)
                for i, rows in enumerate(T0_ROWS):
                    pe.wait_ge(z0_ready, i + 1)
                    mm = nc.tensor.matmul(x1_ps[:, :], w0_sb[0:rows, i, :], z_sb[0:rows, i // 2, i % 2, :],
                                          start=(i == 0), stop=(i == T0 - 1))
                    if i + 4 < T0:
                        select(i + 4)
                mm.then_inc(x1_done, 1)

            slots(pe, slot, first_pairs)


def constants():
    import numpy as np
    one = 0x3F80
    sel = np.zeros((128, SEL_COLS), np.uint16)
    f = np.arange(F0)
    for part in range(PARTS):
        row = f // FQ * XQ + part * FQ + f % FQ
        for s in range(3):
            sel[row, SEL_A + s * F0 + f] = one
        for s in range(SHIFTS):
            sel[row[(f + s) % F0], SEL_B + s * F0 + f] = one
        for field in range(F0):
            sel[row[field], SEL_F + 32 * field:SEL_F + 32 * (field + 1)] = one
        sel[row, SEL_3 + f] = one
    sel[np.arange(128), IDB + np.arange(128)] = one
    eye_mask = np.zeros((128, 128 + SB), np.float32)
    eye_mask[np.arange(128), np.arange(128)] = 1
    eye_mask[np.arange(128), 128 + np.arange(128) % SB] = 1
    return sel, eye_mask


def kernel(dense_ctx, ids, W_top1, b_top1, W_top2, b_top2, W_top3, L0_rec_f0, L0_rec_f1, L0_rec_f2, **tables):
    import numpy as np
    import concourse.bacc as bacc
    from concourse.bass_utils import run_bass_kernel_spmd

    sel, eye_mask = constants()
    f = np.arange(F0)

    def pair_rows(w, mirrored):
        out = np.zeros((3 * F0, T0, MAPS), np.float32)
        for s in range(1 if mirrored else 0, SHIFTS):
            g = (f + s) % F0
            out[s % 3 * F0 + f, s // 3] = w[g * F0 + f if mirrored else f * F0 + g]
        return out

    f0, f1, f2 = (np.asarray(a) for a in (L0_rec_f0, L0_rec_f1, L0_rec_f2))
    padded = np.zeros((4 * FG, MAPS, MAPS), np.float32)
    padded[0:F0] = f1.reshape(F0, MAPS, MAPS)

    def by_groups(a, groups):
        a = np.concatenate([a, np.zeros((len(a), 4 * FQ - F0), np.int32)], axis=1)
        a = a.reshape(-1, 128 // groups, groups, 4 * FQ // groups)
        return a.transpose(2, 1, 0, 3).reshape(128, -1, 4 * FQ // groups)

    sizes = [len(tables[f"tbl_{i}"]) for i in range(F0)]
    table_rows = np.tile(np.array([sum(sizes[:i]) for i in range(F0)], np.int32), (PAIR, 1))
    all_ids = np.asarray(ids)
    arrays = {
        "dense_t": np.asarray(dense_ctx).T,
        "ids_in": by_groups(all_ids, 2),
        "table_rows": by_groups(table_rows, 2),
        "first_ids": by_groups(all_ids[0:PAIR], 4),
        "first_table_rows": by_groups(table_rows[0:CB], 4),
        "tables": np.concatenate([np.asarray(tables[f"tbl_{i}"]) for i in range(F0)]),
        "w0a": pair_rows(f0, False),
        "w0b": pair_rows(f0, True),
        "w1": padded.reshape(FG, 4, GG, 32, MAPS).transpose(1, 3, 0, 2, 4).reshape(128, FG * GG, MAPS),
        "w2": f2.reshape(F0, MAPS, MAPS).transpose(1, 0, 2),
        "wt1": np.asarray(W_top1)[0:3 * MAPS].reshape(3, MAPS, H1).transpose(1, 0, 2),
        "wt1d": np.asarray(W_top1)[3 * MAPS:],
        "wt2": np.asarray(W_top2).reshape(H1 // 128, 128, H2).transpose(1, 0, 2),
        "wt3": np.asarray(W_top3).reshape(H2 // 128, 128).T,
        "bt1": np.asarray(b_top1).reshape(H1 // 128, 128).T,
        "bt2": np.asarray(b_top2).reshape(H2 // 128, 128).T,
        "sel": sel,
        "eye_mask": eye_mask,
    }
    arrays = {"in_" + n: np.ascontiguousarray(a) for n, a in arrays.items()}

    nc = bacc.Bacc("TRN2", target_bir_lowering=False, num_devices=1)
    a = {n: nc.dram_tensor(n, x.shape, mybir.dt.from_np(x.dtype), kind="ExternalInput").ap() for n, x in arrays.items()}
    y = nc.dram_tensor("out_y", (1, B), mybir.dt.float32, kind="ExternalOutput").ap()
    x1_dram = nc.dram_tensor("x1_dram", (2, MAPS, COLS), mybir.dt.float32, kind="Internal").ap()
    dlrm_tower(nc, a["in_dense_t"], a["in_ids_in"], a["in_table_rows"], a["in_first_ids"],
               a["in_first_table_rows"], a["in_tables"], a["in_w0a"], a["in_w0b"],
               a["in_w1"], a["in_w2"], a["in_wt1"], a["in_wt1d"], a["in_wt2"], a["in_wt3"], a["in_bt1"], a["in_bt2"],
               a["in_sel"], a["in_eye_mask"], x1_dram, y)
    r = run_bass_kernel_spmd(nc, [arrays], core_ids=[0])
    return r.results[0]["out_y"].reshape(B, 1)
```
